# Optimizing a Trainium2 kernel written in Bass

```python
import numpy as np
import jax
import jax.numpy as jnp

def _softmax(x, axis=-1):
    return jax.nn.softmax(x, axis=axis)

def _gelu(x):
    return jax.nn.gelu(x, approximate=True)

def _silu(x):
    return jax.nn.silu(x)

def _sigmoid(x):
    return jax.nn.sigmoid(x)

def _layernorm(x, axis=-1, eps=1e-05):
    m = jnp.mean(x, axis=axis, keepdims=True)
    v = jnp.var(x, axis=axis, keepdims=True)
    return (x - m) / jnp.sqrt(v + eps)

def _scatter_add(tgt, idx, src, axis=0):
    return tgt.at[idx].add(src)

def _segment_sum(src, seg, n):
    return jax.ops.segment_sum(src, seg, n)
kernel_name = 'mk_xattn_seq_d2_seqx_r2_8bbab0'

def setup_inputs(seed: int=0):
    np.random.seed(seed)
    _w = jnp.asarray

    def _rec_inputs():
        import jax
        import jax.numpy as jnp
        _rk = jax.random.key(seed)
        x = -0.0002928 + 1 * jax.random.normal(jax.random.fold_in(_rk, 1), (2, 2048, 512), jnp.float32)
        _lenS = 2048 - jax.random.randint(jax.random.fold_in(_rk, 7), (2,), 0, max(1, 2048 // 4) + 1, jnp.int32)
        _lenS2 = 77 - jax.random.randint(jax.random.fold_in(_rk, 8), (2,), 0, max(1, 77 // 4) + 1, jnp.int32)
        _ctx_1024P = jax.random.normal(jax.random.fold_in(_rk, 11), (2, 16, 512), jnp.float32)
        _ctx_1024c = jax.random.dirichlet(jax.random.fold_in(_rk, 511), 0.3 * jnp.ones((16,), jnp.float32), (2, 77))
        _ctx_1024t = jnp.einsum('bsk,bkd->bsd', _ctx_1024c, _ctx_1024P)
        _ctx_1024t = _ctx_1024t * jax.lax.rsqrt(jnp.mean(jnp.square(_ctx_1024t)) + 1e-12) * 0.953939
        ctx_1024 = -1.39393e-06 + 0.999914 * (_ctx_1024t + 0.3 * jax.random.normal(jax.random.fold_in(_rk, 611), (2, 77, 512), jnp.float32))
        return (x, ctx_1024)
    x, ctx_1024 = _rec_inputs()

    def _L0_xattn_setup():
        import jax, jax.numpy as jnp
        import numpy as np
        B, S, D_MODEL, H, D_FF = (2, 1024, 512, 16, 2048)
        D_HEAD = D_MODEL // H
        LN_EPS = 1e-05

        def _xavier(key, shape):
            fan_out, fan_in = shape
            std = (2.0 / (fan_in + fan_out)) ** 0.5
            return jax.random.normal(key, shape, dtype=jnp.float32) * std

        def _layer_norm(x, g, b):
            mu = jnp.mean(x, axis=-1, keepdims=True)
            var = jnp.mean((x - mu) ** 2, axis=-1, keepdims=True)
            return (x - mu) * jax.lax.rsqrt(var + LN_EPS) * g + b
        key = jax.random.key(seed)
        ks = jax.random.split(key, 8)
        return {'q': jax.random.normal(ks[0], (B, S, D_MODEL), dtype=jnp.float32), 'k': jax.random.normal(ks[1], (B, S, D_MODEL), dtype=jnp.float32), 'Wq': _xavier(ks[2], (D_MODEL, D_MODEL)), 'bq': jnp.zeros((D_MODEL,), jnp.float32), 'Wk': _xavier(ks[3], (D_MODEL, D_MODEL)), 'bk': jnp.zeros((D_MODEL,), jnp.float32), 'Wv': _xavier(ks[4], (D_MODEL, D_MODEL)), 'bv': jnp.zeros((D_MODEL,), jnp.float32), 'W1': _xavier(ks[5], (D_FF, D_MODEL)), 'b1': jnp.zeros((D_FF,), jnp.float32), 'W2': _xavier(ks[6], (D_MODEL, D_FF)), 'b2': jnp.zeros((D_MODEL,), jnp.float32), 'ln_g': jnp.ones((D_MODEL,), jnp.float32), 'ln_b': jnp.zeros((D_MODEL,), jnp.float32), 'use_causal_mask': 1}
    _L0_xattn_all = _L0_xattn_setup()
    _L0_xattn_in = {k: v for k, v in _L0_xattn_all.items() if k in ('Wq', 'bq', 'Wk', 'bk', 'Wv', 'bv', 'W1', 'b1', 'W2', 'b2', 'ln_g', 'ln_b')}
    del _L0_xattn_all

    def _L1_xattn_setup():
        import jax, jax.numpy as jnp
        import numpy as np
        B, S, E, H, T, R = (8, 512, 512, 16, 196, 4)
        HD = E // H
        EPS = 1e-05

        def _ln(x, g, b):
            mu = jnp.mean(x, axis=-1, keepdims=True)
            var = jnp.mean(jnp.square(x - mu), axis=-1, keepdims=True)
            return (x - mu) * jax.lax.rsqrt(var + EPS) * g + b

        def _lin(x, w, b):
            return jnp.einsum('bse,oe->bso', x, w) + b

        def _heads(t):
            b, s, _ = t.shape
            return t.reshape(b, s, H, HD).transpose(0, 2, 1, 3)

        def _attend(q, k, v, causal):
            scale = HD ** (-0.5)
            scores = jnp.einsum('bhqd,bhkd->bhqk', q, k) * scale
            if causal:
                sq, sk = (scores.shape[-2], scores.shape[-1])
                mask = jnp.tril(jnp.ones((sq, sk), bool))
                scores = jnp.where(mask, scores, -jnp.inf)
            w = jax.nn.softmax(scores, axis=-1)
            out = jnp.einsum('bhqk,bhkd->bhqd', w, v)
            b, h, s, d = out.shape
            return out.transpose(0, 2, 1, 3).reshape(b, s, h * d)
        key = jax.random.key(seed)
        ks = jax.random.split(key, 12)
        w = lambda k, shape: jax.random.normal(k, shape, jnp.float32) * 0.02
        return {'x': jax.random.normal(ks[0], (B, S, E), jnp.float32), 'enc_out': jax.random.normal(ks[1], (B, T, E), jnp.float32), 'ln1_g': jnp.ones(E), 'ln1_b': jnp.zeros(E), 'attn_qkv_w': w(ks[2], (3 * E, E)), 'attn_qkv_b': jnp.zeros(3 * E), 'attn_proj_w': w(ks[3], (E, E)), 'attn_proj_b': jnp.zeros(E), 'ln2_g': jnp.ones(E), 'ln2_b': jnp.zeros(E), 'q_w': w(ks[4], (E, E)), 'q_b': jnp.zeros(E), 'k_w': w(ks[5], (E, E)), 'k_b': jnp.zeros(E), 'v_w': w(ks[6], (E, E)), 'v_b': jnp.zeros(E), 'ca_proj_w': w(ks[7], (E, E)), 'ca_proj_b': jnp.zeros(E), 'ln3_g': jnp.ones(E), 'ln3_b': jnp.zeros(E), 'fc_w': w(ks[8], (R * E, E)), 'fc_b': jnp.zeros(R * E), 'proj_w': w(ks[9], (E, R * E)), 'proj_b': jnp.zeros(E)}
    _L1_xattn_all = _L1_xattn_setup()
    _L1_xattn_in = {k: v for k, v in _L1_xattn_all.items() if k in ('ln1_g', 'ln1_b', 'attn_qkv_w', 'attn_qkv_b', 'attn_proj_w', 'attn_proj_b', 'ln2_g', 'ln2_b', 'q_w', 'q_b', 'k_w', 'k_b', 'v_w', 'v_b', 'ca_proj_w', 'ca_proj_b', 'ln3_g', 'ln3_b', 'fc_w', 'fc_b', 'proj_w', 'proj_b')}
    del _L1_xattn_all
    return {'x': x, 'ctx_1024': ctx_1024, 'L0_xattn_Wq': _L0_xattn_in['Wq'], 'L0_xattn_bq': _L0_xattn_in['bq'], 'L0_xattn_Wk': _L0_xattn_in['Wk'], 'L0_xattn_bk': _L0_xattn_in['bk'], 'L0_xattn_Wv': _L0_xattn_in['Wv'], 'L0_xattn_bv': _L0_xattn_in['bv'], 'L0_xattn_W1': _L0_xattn_in['W1'], 'L0_xattn_b1': _L0_xattn_in['b1'], 'L0_xattn_W2': _L0_xattn_in['W2'], 'L0_xattn_b2': _L0_xattn_in['b2'], 'L0_xattn_ln_g': _L0_xattn_in['ln_g'], 'L0_xattn_ln_b': _L0_xattn_in['ln_b'], 'L1_xattn_ln1_g': _L1_xattn_in['ln1_g'], 'L1_xattn_ln1_b': _L1_xattn_in['ln1_b'], 'L1_xattn_attn_qkv_w': _L1_xattn_in['attn_qkv_w'], 'L1_xattn_attn_qkv_b': _L1_xattn_in['attn_qkv_b'], 'L1_xattn_attn_proj_w': _L1_xattn_in['attn_proj_w'], 'L1_xattn_attn_proj_b': _L1_xattn_in['attn_proj_b'], 'L1_xattn_ln2_g': _L1_xattn_in['ln2_g'], 'L1_xattn_ln2_b': _L1_xattn_in['ln2_b'], 'L1_xattn_q_w': _L1_xattn_in['q_w'], 'L1_xattn_q_b': _L1_xattn_in['q_b'], 'L1_xattn_k_w': _L1_xattn_in['k_w'], 'L1_xattn_k_b': _L1_xattn_in['k_b'], 'L1_xattn_v_w': _L1_xattn_in['v_w'], 'L1_xattn_v_b': _L1_xattn_in['v_b'], 'L1_xattn_ca_proj_w': _L1_xattn_in['ca_proj_w'], 'L1_xattn_ca_proj_b': _L1_xattn_in['ca_proj_b'], 'L1_xattn_ln3_g': _L1_xattn_in['ln3_g'], 'L1_xattn_ln3_b': _L1_xattn_in['ln3_b'], 'L1_xattn_fc_w': _L1_xattn_in['fc_w'], 'L1_xattn_fc_b': _L1_xattn_in['fc_b'], 'L1_xattn_proj_w': _L1_xattn_in['proj_w'], 'L1_xattn_proj_b': _L1_xattn_in['proj_b']}

def reference(x, ctx_1024, L0_xattn_Wq, L0_xattn_bq, L0_xattn_Wk, L0_xattn_bk, L0_xattn_Wv, L0_xattn_bv, L0_xattn_W1, L0_xattn_b1, L0_xattn_W2, L0_xattn_b2, L0_xattn_ln_g, L0_xattn_ln_b, L1_xattn_ln1_g, L1_xattn_ln1_b, L1_xattn_attn_qkv_w, L1_xattn_attn_qkv_b, L1_xattn_attn_proj_w, L1_xattn_attn_proj_b, L1_xattn_ln2_g, L1_xattn_ln2_b, L1_xattn_q_w, L1_xattn_q_b, L1_xattn_k_w, L1_xattn_k_b, L1_xattn_v_w, L1_xattn_v_b, L1_xattn_ca_proj_w, L1_xattn_ca_proj_b, L1_xattn_ln3_g, L1_xattn_ln3_b, L1_xattn_fc_w, L1_xattn_fc_b, L1_xattn_proj_w, L1_xattn_proj_b):
    import jax
    import jax.numpy as jnp

    def _L0_xattn_ref(q, k, Wq, bq, Wk, bk, Wv, bv, W1, b1, W2, b2, ln_g, ln_b, use_causal_mask):
        import jax, jax.numpy as jnp
        import numpy as np
        B, S, D_MODEL, H, D_FF = (2, 1024, 512, 16, 2048)
        D_HEAD = D_MODEL // H
        LN_EPS = 1e-05

        def _xavier(key, shape):
            fan_out, fan_in = shape
            std = (2.0 / (fan_in + fan_out)) ** 0.5
            return jax.random.normal(key, shape, dtype=jnp.float32) * std

        def _layer_norm(x, g, b):
            mu = jnp.mean(x, axis=-1, keepdims=True)
            var = jnp.mean((x - mu) ** 2, axis=-1, keepdims=True)
            return (x - mu) * jax.lax.rsqrt(var + LN_EPS) * g + b
        Bq, Sq, _ = q.shape
        Sk = k.shape[1]
        Q = q @ Wq.T + bq
        K = k @ Wk.T + bk
        V = k @ Wv.T + bv
        Q_ = Q.reshape(Bq, Sq, H, D_HEAD).transpose(0, 2, 1, 3)
        K_ = K.reshape(Bq, Sk, H, D_HEAD).transpose(0, 2, 1, 3)
        V_ = V.reshape(Bq, Sk, H, D_HEAD).transpose(0, 2, 1, 3)
        scores = jnp.einsum('bhqd,bhkd->bhqk', Q_, K_) / D_HEAD ** 0.5
        if use_causal_mask:
            causal = jnp.tril(jnp.ones((Sq, Sk), dtype=bool))
            scores = jnp.where(causal, scores, jnp.float32(-1000000000.0))
        sim = jax.nn.softmax(scores, axis=-1)
        att = jnp.einsum('bhqk,bhkd->bhqd', sim, V_)
        att_h = att.transpose(0, 2, 1, 3).reshape(Bq, Sq, D_MODEL)
        att_h = att_h + q
        att_h = _layer_norm(att_h, ln_g, ln_b)
        ff = jax.nn.gelu(att_h @ W1.T + b1, approximate=False) @ W2.T + b2
        return ff + att_h

    def _L1_xattn_ref(x, enc_out, ln1_g, ln1_b, attn_qkv_w, attn_qkv_b, attn_proj_w, attn_proj_b, ln2_g, ln2_b, q_w, q_b, k_w, k_b, v_w, v_b, ca_proj_w, ca_proj_b, ln3_g, ln3_b, fc_w, fc_b, proj_w, proj_b):
        import jax, jax.numpy as jnp
        import numpy as np
        B, S, E, H, T, R = (8, 512, 512, 16, 196, 4)
        HD = E // H
        EPS = 1e-05

        def _ln(x, g, b):
            mu = jnp.mean(x, axis=-1, keepdims=True)
            var = jnp.mean(jnp.square(x - mu), axis=-1, keepdims=True)
            return (x - mu) * jax.lax.rsqrt(var + EPS) * g + b

        def _lin(x, w, b):
            return jnp.einsum('bse,oe->bso', x, w) + b

        def _heads(t):
            b, s, _ = t.shape
            return t.reshape(b, s, H, HD).transpose(0, 2, 1, 3)

        def _attend(q, k, v, causal):
            scale = HD ** (-0.5)
            scores = jnp.einsum('bhqd,bhkd->bhqk', q, k) * scale
            if causal:
                sq, sk = (scores.shape[-2], scores.shape[-1])
                mask = jnp.tril(jnp.ones((sq, sk), bool))
                scores = jnp.where(mask, scores, -jnp.inf)
            w = jax.nn.softmax(scores, axis=-1)
            out = jnp.einsum('bhqk,bhkd->bhqd', w, v)
            b, h, s, d = out.shape
            return out.transpose(0, 2, 1, 3).reshape(b, s, h * d)
        h = _ln(x, ln1_g, ln1_b)
        qkv = _lin(h, attn_qkv_w, attn_qkv_b)
        q, k, v = jnp.split(qkv, 3, axis=-1)
        a = _attend(_heads(q), _heads(k), _heads(v), causal=True)
        x = x + _lin(a, attn_proj_w, attn_proj_b)
        h = _ln(x, ln2_g, ln2_b)
        q = _heads(_lin(h, q_w, q_b))
        k = _heads(_lin(enc_out, k_w, k_b))
        v = _heads(_lin(enc_out, v_w, v_b))
        a = _attend(q, k, v, causal=False)
        x = x + _lin(a, ca_proj_w, ca_proj_b)
        h = _ln(x, ln3_g, ln3_b)
        h = jax.nn.gelu(_lin(h, fc_w, fc_b), approximate=False)
        x = x + _lin(h, proj_w, proj_b)
        return x
    x = _L0_xattn_ref(x, ctx_1024, L0_xattn_Wq, L0_xattn_bq, L0_xattn_Wk, L0_xattn_bk, L0_xattn_Wv, L0_xattn_bv, L0_xattn_W1, L0_xattn_b1, L0_xattn_W2, L0_xattn_b2, L0_xattn_ln_g, L0_xattn_ln_b, 1)
    x = _L1_xattn_ref(x, ctx_1024, L1_xattn_ln1_g, L1_xattn_ln1_b, L1_xattn_attn_qkv_w, L1_xattn_attn_qkv_b, L1_xattn_attn_proj_w, L1_xattn_attn_proj_b, L1_xattn_ln2_g, L1_xattn_ln2_b, L1_xattn_q_w, L1_xattn_q_b, L1_xattn_k_w, L1_xattn_k_b, L1_xattn_v_w, L1_xattn_v_b, L1_xattn_ca_proj_w, L1_xattn_ca_proj_b, L1_xattn_ln3_g, L1_xattn_ln3_b, L1_xattn_fc_w, L1_xattn_fc_b, L1_xattn_proj_w, L1_xattn_proj_b)
    return x

_drawn_inputs = setup_inputs


def setup_inputs(seed=0):
    import zlib

    import numpy as np

    out = dict(_drawn_inputs(seed))
    spreads = {'L0_xattn_bq': (0.0, 0.375),
     'L0_xattn_bk': (0.0, 0.8),
     'L0_xattn_bv': (0.0, 0.1),
     'L0_xattn_b1': (0.0, 0.1),
     'L0_xattn_b2': (0.0, 0.1),
     'L0_xattn_ln_g': (1.0, 0.2),
     'L0_xattn_ln_b': (0.0, 0.1),
     'L1_xattn_ln1_g': (1.0, 0.6),
     'L1_xattn_ln1_b': (0.0, 0.496),
     'L1_xattn_attn_qkv_b': (0.0, 0.1),
     'L1_xattn_attn_proj_b': (0.0, 0.1),
     'L1_xattn_ln2_g': (1.0, 0.6),
     'L1_xattn_ln2_b': (0.0, 0.8),
     'L1_xattn_q_b': (0.0, 0.8),
     'L1_xattn_k_b': (0.0, 0.8),
     'L1_xattn_v_b': (0.0, 0.1),
     'L1_xattn_ca_proj_b': (0.0, 0.1),
     'L1_xattn_ln3_g': (1.0, 0.2),
     'L1_xattn_ln3_b': (0.0, 0.417),
     'L1_xattn_fc_b': (0.0, 0.1),
     'L1_xattn_proj_b': (0.0, 0.1)}
    factors = {'L1_xattn_q_w': 7.737, 'L1_xattn_k_w': 7.508}
    for name, (base, spread) in spreads.items():
        noise = np.random.default_rng([zlib.crc32(name.encode()), seed]).standard_normal(out[name].shape)
        drawn = base * np.exp(spread * noise) if base else spread * noise
        out[name] = jnp.asarray(drawn.astype(out[name].dtype))
    for name, factor in factors.items():
        out[name] = (out[name] * factor).astype(out[name].dtype)
    return out
```

```python
from contextlib import ExitStack

import concourse.bass as bass
from concourse import mybir

F32 = mybir.dt.float32
F32R = mybir.dt.float32r
BF16 = mybir.dt.bfloat16
ALU = mybir.AluOpType
ACT = mybir.ActivationFunctionType
AX_X = mybir.AxisListType.X

P = 128
B, S, D = 2, 2048, 512
H = 16
DH = D // H
SK = 77
DFF = 2048
TOK = B * S
KT = D // P
G = D // P
HG = H // G
CH = 512
NCH = TOK // CH
TT = CH // P
FT = DFF // P
CPB = S // CH
KEYS = HG * SK
SCALE = float(DH) ** -0.5
EPS = 1e-5
MASKED = -1e30
BANK = 512


def wait(eng, sem, value):
    if not isinstance(value, int) or value > 0:
        eng.wait_ge(sem, value)


def over_chunks(eng, body, count=NCH):
    body(0, 0, 0)
    with eng.Fori(0, (count - 2) // 2) as i:
        body(2 * i + 1, 1, i)
        body(2 * i + 2, 0, i + 1)
    body(count - 1, 1, count // 2 - 1)


def not_first(n):
    return not (isinstance(n, int) and n == 0)


def not_last(n, count=NCH):
    return not (isinstance(n, int) and n == count - 1)


def raw32(ap):
    return ap.bitcast(F32)


def mm3(pe, out, w_hi, w_lo, x_hi, x_lo, start, stop):
    pe.matmul(out, w_hi, x_hi, start=start, stop=False)
    pe.matmul(out, w_hi, x_lo, start=False, stop=False)
    return pe.matmul(out, w_lo, x_hi, start=False, stop=stop)


class Stage:

    def __init__(self, nc, tag, ctx):
        self.nc, self.tag, self.ctx, self.sems = nc, tag, ctx, []

    def sb(self, name, shape, dt=F32):
        return self.ctx.enter_context(self.nc.sbuf_tensor(f"{self.tag}_{name}", shape, dt))

    def psum(self, name, shape):
        return self.ctx.enter_context(self.nc.psum_tensor(f"{self.tag}_{name}", shape, F32))

    def sem(self, name):
        s = self.nc.alloc_semaphore(f"{self.tag}_{name}")
        self.sems.append(s)
        return s

    def close(self):
        self.nc.clear_and_free_semaphores(self.sems)
        self.nc.all_engine_barrier()



def build_constants(nc, ctx, c):
    def sb(name, shape, dt=F32):
        return ctx.enter_context(nc.sbuf_tensor(name, shape, dt))

    c["ident"] = sb("ident", [P, P])
    c["ident_bf"] = sb("ident_bf", [P, P], BF16)
    c["half_neg"] = sb("half_neg", [P, TT])
    c["eps"] = sb("eps", [P, TT])
    with ExitStack() as own:
        st = Stage(nc, "const", own)
        made = st.sem("made")
        with nc.Block() as block:
            @block.gpsimd
            def _(pool):
                pool.memset(c["ident"][:, :], 0.0).then_inc(made, 1)
                pool.wait_ge(made, 1)
                pool.affine_select(out=c["ident"][:, :], in_=c["ident"][:, :], compare_op=ALU.not_equal,
                                   fill=1.0, base=0, pattern=[[-1, P]], channel_multiplier=1).then_inc(made, 1)
                pool.wait_ge(made, 2)
                pool.tensor_copy(c["ident_bf"][:, :], c["ident"][:, :]).then_inc(made, 1)
                pool.memset(c["half_neg"][:, :], -0.5).then_inc(made, 1)
                pool.memset(c["eps"][:, :], EPS).then_inc(made, 1)
                pool.wait_ge(made, 5)
        st.close()



class LnTail:

    def __init__(self, st, c, gain, shift, out_t):
        self.c, self.gain, self.shift, self.out_t = c, gain, shift, out_t
        self.stats = st.sb("stats", [P, TT, 6])
        self.mv = st.sb("mv", [P, TT, 2])
        self.veps = st.sb("veps", [P, TT, 1])
        self.rstd = st.sb("rstd", [P, TT])
        self.spacer = st.sb("spacer", [P, 1])
        self.z = st.sb("z", [P, TT, D])
        self.out = st.sb("ln_out", [P, 2, CH])
        self.psum = st.psum("ln_psum", [P, 2, BANK])
        self.stats_made = st.sem("stats_made")
        self.mv_made = st.sem("mv_made")
        self.veps_made = st.sem("veps_made")
        self.rstd_made = st.sem("rstd_made")
        self.z_made = st.sem("z_made")
        self.turned = st.sem("turned")
        self.evacuated = st.sem("evacuated")
        self.stored = [st.sem(f"ln_stored{i}") for i in range(2)]

    def dve_stats(self, dve, y, n):
        for t in range(TT):
            dve.bn_stats(self.stats[:, t, :], y[:, t, :]).then_inc(self.stats_made, 1)
        wait(dve, self.stats_made, n * TT + TT)
        dve.memset(self.spacer[:, :], 0.0)
        for t in range(TT):
            dve.bn_aggr(self.mv[:, t, :], self.stats[:, t, :]).then_inc(self.mv_made, 1)

    def pool_rstd(self, pool, n):
        wait(pool, self.mv_made, n * TT + TT)
        if not_first(n):
            wait(pool, self.z_made, n * TT)
        pool.tensor_tensor(self.veps[:, :, :], self.mv[:, :, 1:2], self.c["eps"][:, :].unsqueeze(2),
                           ALU.add).then_inc(self.veps_made, 1)
        wait(pool, self.veps_made, n + 1)
        pool.tensor_tensor(self.rstd[:, :], self.veps[:, :, 0], self.c["half_neg"][:, :],
                           ALU.pow).then_inc(self.rstd_made, 1)

    def dve_z(self, dve, y, n):
        wait(dve, self.rstd_made, n + 1)
        if not_first(n):
            wait(dve, self.turned, n * KT)
        for t in range(TT):
            dve.tensor_scalar(self.z[:, t, :], y[:, t, :], self.mv[:, t, 0:1], self.rstd[:, t:t + 1],
                              ALU.subtract, ALU.mult).then_inc(self.z_made, 1)

    def pe_turn(self, pe, n):
        wait(pe, self.z_made, n * TT + TT)
        for ft in range(KT):
            wait(pe, self.evacuated, n * KT + ft + 1)
            for t in range(TT):
                last = pe.transpose(self.psum[:, ft % 2, t * P:(t + 1) * P],
                                    self.z[:, t, ft * P:(ft + 1) * P], self.c["ident"][:, :])
            last.then_inc(self.turned, 1)

    def act_credit(self, act):
        act.sem_inc(self.evacuated, 2)

    def act_out(self, act, n):
        for ft in range(KT):
            wait(act, self.turned, n * KT + ft + 1)
            wait(act, self.stored[ft % 2], (n * 2 + ft // 2 + 1) * 16)
            act.activation(self.out[:, ft % 2, :], self.psum[:, ft % 2, :], ACT.Identity,
                           bias=self.shift[:, ft:ft + 1],
                           scale=self.gain[:, ft:ft + 1]).then_inc(self.evacuated, 1)

    def sp_credit(self, sp):
        for s in self.stored:
            sp.sem_inc(s, 16)

    def sp_store(self, sp, n):
        for ft in range(KT):
            wait(sp, self.evacuated, n * KT + ft + 3)
            sp.dma_start(self.out_t[:, ft, bass.ds(n * CH, CH)],
                         self.out[:, ft % 2, :]).then_inc(self.stored[ft % 2], 16)

    def sp_drain(self, sp):
        for s in self.stored:
            sp.wait_ge(s, NCH * 2 * 16 + 16)


class SplitInput:

    def __init__(self, st, src, slots, slot_free, name="x"):
        self.src, self.slots = src, slots
        self.slot_free = slot_free
        self.raw = st.sb(f"{name}_raw", [P, 2, CH])
        self.hi = st.sb(f"{name}_hi", [P, slots, KT, CH], F32R)
        self.lo = st.sb(f"{name}_lo", [P, slots, KT, CH], F32R)
        self.loaded = [st.sem(f"{name}_loaded{i}") for i in range(2)]
        self.hi_made = st.sem(f"{name}_hi_made")
        self.lo_made = st.sem(f"{name}_lo_made")

    def sp_load(self, sp, n):
        for kt in range(KT):
            wait(sp, self.lo_made, n * KT + kt + 1)
            sp.dma_start(self.raw[:, kt % 2, :],
                         self.src[:, kt, bass.ds(n * CH, CH)]).then_inc(self.loaded[kt % 2], 16)

    def make_hi(self, eng, copy, n, u):
        self.slot_free(eng, n)
        for kt in range(KT):
            wait(eng, self.loaded[kt % 2], (n * 2 + kt // 2 + 1) * 16)
            copy(self.hi[:, u % self.slots, kt, :], self.raw[:, kt % 2, :]).then_inc(self.hi_made, 1)

    def lo_credit(self, eng):
        eng.sem_inc(self.lo_made, 2)

    def make_lo(self, eng, n, u):
        for kt in range(KT):
            wait(eng, self.hi_made, n * KT + kt + 1)
            eng.tensor_tensor(self.lo[:, u % self.slots, kt, :], self.raw[:, kt % 2, :],
                              raw32(self.hi[:, u % self.slots, kt, :]),
                              ALU.subtract).then_inc(self.lo_made, 1)

    def make_both(self, eng, n, u):
        self.slot_free(eng, n)
        for kt in range(KT):
            wait(eng, self.loaded[kt % 2], (n * 2 + kt // 2 + 1) * 16)
            eng.tensor_copy(self.hi[:, u % self.slots, kt, :],
                            self.raw[:, kt % 2, :]).then_inc(self.hi_made, 1)
            wait(eng, self.hi_made, n * KT + kt + 1)
            eng.tensor_tensor(self.lo[:, u % self.slots, kt, :], self.raw[:, kt % 2, :],
                              raw32(self.hi[:, u % self.slots, kt, :]),
                              ALU.subtract).then_inc(self.lo_made, 1)

    def pe_ready(self, pe, n):
        wait(pe, self.lo_made, n * KT + KT + 2)

    def halves(self, u, kt, cols):
        u = u % self.slots
        return self.hi[:, u, kt, cols], self.lo[:, u, kt, cols]


class Weights:
    PIECE = 512

    def __init__(self, st, pieces, name="w"):
        self.pieces = pieces
        n = len(pieces)
        self.raw = st.sb(f"{name}_raw", [P, 2, self.PIECE])
        self.hi = st.sb(f"{name}_hi", [P, n, self.PIECE], F32R)
        self.lo = st.sb(f"{name}_lo", [P, n, self.PIECE], F32R)
        self.loaded = [st.sem(f"{name}_loaded{i}") for i in range(2)]
        self.hi_made = st.sem(f"{name}_hi_made")
        self.lo_made = st.sem(f"{name}_lo_made")

    def sp_load(self, sp, first=0, last=None):
        for k in range(first, len(self.pieces) if last is None else last):
            wait(sp, self.lo_made, k - 1)
            sp.dma_start(self.raw[:, k % 2, :], self.pieces[k]).then_inc(self.loaded[k % 2], 16)

    def make_hi(self, eng, copy):
        for k in range(len(self.pieces)):
            eng.wait_ge(self.loaded[k % 2], (k // 2 + 1) * 16)
            copy(self.hi[:, k, :], self.raw[:, k % 2, :]).then_inc(self.hi_made, 1)

    def make_lo(self, eng):
        for k in range(len(self.pieces)):
            eng.wait_ge(self.hi_made, k + 1)
            eng.tensor_tensor(self.lo[:, k, :], self.raw[:, k % 2, :], raw32(self.hi[:, k, :]),
                              ALU.subtract).then_inc(self.lo_made, 1)

    def make_both(self, eng):
        for k in range(len(self.pieces)):
            eng.wait_ge(self.loaded[k % 2], (k // 2 + 1) * 16)
            eng.tensor_copy(self.hi[:, k, :], self.raw[:, k % 2, :]).then_inc(self.hi_made, 1)
            eng.wait_ge(self.hi_made, k + 1)
            eng.tensor_tensor(self.lo[:, k, :], self.raw[:, k % 2, :], raw32(self.hi[:, k, :]),
                              ALU.subtract).then_inc(self.lo_made, 1)

    def halves(self, k, cols=slice(0, 512)):
        return self.hi[:, k, cols], self.lo[:, k, cols]


def load_columns(nc, ctx, d, c):
    cols = ctx.enter_context(nc.sbuf_tensor("vector_columns", [P, d["columns"].shape[1]], F32))
    c["cols"] = cols
    with ExitStack() as own:
        st = Stage(nc, "cols", own)
        loaded = st.sem("loaded")
        with nc.Block() as block:
            @block.sync
            def _(sp):
                sp.dma_start(cols[:, :], d["columns"]).then_inc(loaded, 16)
                sp.wait_ge(loaded, 16)
        st.close()



def stage_ff(nc, tag, c, x_t, residual, w1, w2, b1, b2_row, y_out, norm=None):
    with ExitStack() as ctx:
        st = Stage(nc, tag, ctx)
        up_done = st.sem("up_done")
        x = SplitInput(st, x_t, 1, lambda eng, n: wait(eng, up_done, n * FT))
        w = Weights(st, [piece for j in range(FT) for piece in (w1[j], w2[j])])
        ln = LnTail(st, c, norm[0], norm[1], norm[2]) if norm else None
        act_out = st.sb("act_out", [P, 2, CH])
        h_hi = st.sb("h_hi", [P, 4, CH], F32R)
        h_lo = st.sb("h_lo", [P, 4, CH], F32R)
        y = st.sb("y", [P, 2, TT, D])
        b2 = st.sb("b2", [P, D])
        up = st.psum("up", [P, 2, BANK])
        acc = st.psum("acc", [P, TT, BANK])

        b2_loaded = st.sem("b2_loaded")
        res_loaded = [st.sem(f"res_loaded{i}") for i in range(2)]
        res_biased = st.sem("res_biased")
        gelu_done = st.sem("gelu_done")
        hi_done = st.sem("hi_done")
        lo_done = st.sem("lo_done")
        down_done = st.sem("down_done")
        y_done = st.sem("y_done")
        y_stored = [st.sem(f"y_stored{i}") for i in range(2)]

        with nc.Block() as block:
            @block.sync
            def _(sp):
                def load_residual(n, u, use):
                    wait(sp, y_stored[u], use * 16)
                    if ln and not (isinstance(n, int) and n < 2):
                        wait(sp, ln.z_made, (n - 1) * TT)
                    sp.dma_start(y[:, u], residual[:, bass.ds(n * TT, TT), :]).then_inc(res_loaded[u], 16)

                if ln:
                    ln.sp_credit(sp)
                sp.dma_start(b2[:, :], b2_row).then_inc(b2_loaded, 16)
                x.sp_load(sp, 0)
                w.sp_load(sp)
                load_residual(0, 0, 0)

                def body(n, u, use):
                    if ln and not_first(n):
                        ln.sp_store(sp, n - 1)
                    if not_last(n):
                        load_residual(n + 1, 1 - u, use + u)
                        x.sp_load(sp, n + 1)
                    wait(sp, y_done, n * TT + TT)
                    sp.dma_start(y_out[:, bass.ds(n * TT, TT), :], y[:, u]).then_inc(y_stored[u], 16)
                over_chunks(sp, body)
                if ln:
                    ln.sp_store(sp, NCH - 1)
                    ln.sp_drain(sp)
                for s in y_stored:
                    sp.wait_ge(s, NCH // 2 * 16)

            @block.gpsimd
            def _(pool):
                w.make_both(pool)
                pool.wait_ge(b2_loaded, 16)

                def body(n, u, use):
                    wait(pool, res_loaded[u], (use + 1) * 16)
                    pool.tensor_tensor(y[:, u], y[:, u], b2[:, :].unsqueeze(1).to_broadcast([P, TT, D]),
                                       ALU.add).then_inc(res_biased, 1)
                    if ln and not_first(n):
                        ln.pool_rstd(pool, n - 1)
                over_chunks(pool, body)
                if ln:
                    ln.pool_rstd(pool, NCH - 1)

            @block.scalar
            def _(act):
                if ln:
                    ln.act_credit(act)

                def body(n, u, use):
                    for j in range(FT):
                        wait(act, up_done, n * FT + j + 1)
                        wait(act, lo_done, n * FT + j - 1)
                        act.activation(act_out[:, j % 2, :], up[:, j % 2, :], ACT.Gelu,
                                       bias=b1[:, j:j + 1]).then_inc(gelu_done, 1)
                        if ln and j == 8 and not_first(n):
                            ln.act_out(act, n - 1)
                over_chunks(act, body)
                if ln:
                    ln.act_out(act, NCH - 1)

            @block.vector
            def _(dve):
                x.lo_credit(dve)
                x.make_both(dve, 0, 0)

                def body(n, u, use):
                    for j in range(FT):
                        wait(dve, gelu_done, n * FT + j + 1)
                        wait(dve, down_done, n * FT + j - 3)
                        dve.tensor_copy(h_hi[:, j % 4, :], act_out[:, j % 2, :]).then_inc(hi_done, 1)
                        wait(dve, hi_done, n * FT + j + 1)
                        dve.tensor_tensor(h_lo[:, j % 4, :], act_out[:, j % 2, :], raw32(h_hi[:, j % 4, :]),
                                          ALU.subtract).then_inc(lo_done, 1)
                        if ln and j == 1 and not_first(n):
                            ln.dve_stats(dve, y[:, 1 - u], n - 1)
                        if ln and j == 4 and not_first(n):
                            ln.dve_z(dve, y[:, 1 - u], n - 1)
                    if not_last(n):
                        x.make_both(dve, n + 1, 0)
                    wait(dve, down_done, n * FT + FT)
                    wait(dve, res_biased, n + 1)
                    for t in range(TT):
                        dve.tensor_tensor(y[:, u, t, :], acc[:, t, :], y[:, u, t, :], ALU.add).then_inc(y_done, 1)
                over_chunks(dve, body)
                if ln:
                    wait(dve, y_done, NCH * TT)
                    ln.dve_stats(dve, y[:, 1], NCH - 1)
                    ln.dve_z(dve, y[:, 1], NCH - 1)

            @block.tensor
            def _(pe):
                def up_tile(n, j):
                    if j == 0:
                        x.pe_ready(pe, n)
                    if isinstance(n, int) and n == 0:
                        wait(pe, w.lo_made, 2 * j + 1)
                    wait(pe, gelu_done, n * FT + j - 1)
                    for kt in range(KT):
                        last = mm3(pe, up[:, j % 2, :], *w.halves(2 * j, slice(kt * P, kt * P + P)),
                                   *x.halves(0, kt, slice(0, CH)), start=(kt == 0), stop=(kt == KT - 1))
                    last.then_inc(up_done, 1)

                def down_tile(n, j):
                    wait(pe, lo_done, n * FT + j + 1)
                    if isinstance(n, int) and n == 0:
                        wait(pe, w.lo_made, 2 * j + 2)
                    if j == 0:
                        wait(pe, y_done, n * TT)
                    for t in range(TT):
                        cols = slice(t * P, t * P + P)
                        last = mm3(pe, acc[:, t, :], h_hi[:, j % 4, cols], h_lo[:, j % 4, cols],
                                   *w.halves(2 * j + 1), start=(j == 0), stop=(j == FT - 1))
                    last.then_inc(down_done, 1)

                def body(n, u, use):
                    for j in range(FT):
                        up_tile(n, j)
                        if ln and j == 8 and not_first(n):
                            ln.pe_turn(pe, n - 1)
                        if j >= 2:
                            down_tile(n, j - 2)
                    down_tile(n, FT - 2)
                    down_tile(n, FT - 1)
                over_chunks(pe, body)
                if ln:
                    ln.pe_turn(pe, NCH - 1)
        st.close()



def stage_merge(nc, tag, c, att_t, residual, norm, y_out, w=None, bias_row=None, norm_rows=None):
    with ExitStack() as ctx:
        st = Stage(nc, tag, ctx)
        summed = st.sem("summed")
        ln = LnTail(st, c, norm[0], norm[1], norm[2])
        acc = st.psum("acc", [P, TT, BANK])
        y = st.sb("y", [P, 2, TT, D])
        row = st.sb("row", [P, 2, D])
        res_loaded = [st.sem(f"res_loaded{i}") for i in range(2)]
        row_loaded = st.sem("row_loaded")
        res_biased = st.sem("res_biased")
        y_done = st.sem("y_done")
        y_stored = [st.sem(f"y_stored{i}") for i in range(2)]
        if w is not None:
            x = SplitInput(st, att_t, 2, lambda eng, n: wait(eng, summed, n * TT + TT))
            weights = Weights(st, w)
        else:
            att = st.sb("att", [P, 2, KT, CH])
            att_loaded = [st.sem(f"att_loaded{i}") for i in range(2)]
        if norm_rows is not None:
            normed = st.sb("normed", [P, TT, D])
            gained = st.sem("gained")
            shifted = st.sem("shifted")
            normed_stored = st.sem("normed_stored")

        with nc.Block() as block:
            @block.sync
            def _(sp):
                def load_residual(n, u, use):
                    if norm_rows is None:
                        wait(sp, y_stored[u], use * 16)
                    if not (isinstance(n, int) and n < 2):
                        wait(sp, ln.z_made, (n - 1) * TT)
                    sp.dma_start(y[:, u], residual[:, bass.ds(n * TT, TT), :]).then_inc(res_loaded[u], 16)

                def load_att(n, u, use):
                    wait(sp, summed, n * TT + TT)
                    sp.dma_start(att[:, u], att_t[:, :, bass.ds(n * CH, CH)]).then_inc(att_loaded[u], 16)

                ln.sp_credit(sp)
                rows = norm_rows if norm_rows is not None else (bias_row,)
                for r, src in enumerate(rows):
                    sp.dma_start(row[:, r, :], src).then_inc(row_loaded, 16)
                if w is not None:
                    weights.sp_load(sp)
                    x.sp_load(sp, 0)
                else:
                    load_att(0, 0, 0)
                load_residual(0, 0, 0)

                def body(n, u, use):
                    if not_last(n):
                        load_residual(n + 1, 1 - u, use + u)
                        if w is not None:
                            x.sp_load(sp, n + 1)
                        else:
                            load_att(n + 1, 1 - u, use + u)
                    if not_first(n):
                        ln.sp_store(sp, n - 1)
                        if norm_rows is not None:
                            wait(sp, shifted, n)
                            sp.dma_start(y_out[:, bass.ds((n - 1) * TT, TT), :],
                                         normed[:, :, :]).then_inc(normed_stored, 16)
                    if norm_rows is None:
                        wait(sp, y_done, n * TT + TT)
                        sp.dma_start(y_out[:, bass.ds(n * TT, TT), :], y[:, u]).then_inc(y_stored[u], 16)
                over_chunks(sp, body)
                ln.sp_store(sp, NCH - 1)
                ln.sp_drain(sp)
                if norm_rows is not None:
                    wait(sp, shifted, NCH)
                    sp.dma_start(y_out[:, (NCH - 1) * TT:NCH * TT, :], normed[:, :, :]).then_inc(normed_stored, 16)
                    sp.wait_ge(normed_stored, NCH * 16)
                else:
                    for s in y_stored:
                        sp.wait_ge(s, NCH // 2 * 16)

            @block.gpsimd
            def _(pool):
                pool.wait_ge(row_loaded, 16 * (2 if norm_rows is not None else 1))
                if w is not None:
                    x.lo_credit(pool)
                    x.make_lo(pool, 0, 0)

                def row_of(r):
                    return row[:, r, :].unsqueeze(1).to_broadcast([P, TT, D])

                def body(n, u, use):
                    if w is not None:
                        wait(pool, res_loaded[u], (use + 1) * 16)
                        pool.tensor_tensor(y[:, u], y[:, u], row_of(0), ALU.add).then_inc(res_biased, 1)
                        if not_last(n):
                            x.make_lo(pool, n + 1, 1 - u)
                    ln.pool_rstd(pool, n)
                    if norm_rows is not None:
                        wait(pool, ln.z_made, n * TT + TT)
                        wait(pool, normed_stored, n * 16)
                        pool.tensor_tensor(normed[:, :, :], ln.z[:, :, :], row_of(0), ALU.mult).then_inc(gained, 1)
                        wait(pool, gained, n + 1)
                        pool.tensor_tensor(normed[:, :, :], normed[:, :, :], row_of(1),
                                           ALU.add).then_inc(shifted, 1)
                over_chunks(pool, body)

            @block.scalar
            def _(act):
                ln.act_credit(act)
                if w is not None:
                    weights.make_hi(act, act.copy)
                    x.make_hi(act, act.copy, 0, 0)

                def body(n, u, use):
                    if w is not None and not_last(n):
                        x.make_hi(act, act.copy, n + 1, 1 - u)
                    if not_first(n):
                        ln.act_out(act, n - 1)
                over_chunks(act, body)
                ln.act_out(act, NCH - 1)

            @block.vector
            def _(dve):
                if w is not None:
                    weights.make_lo(dve)

                def body(n, u, use):
                    if w is not None:
                        wait(dve, res_biased, n + 1)
                    else:
                        wait(dve, res_loaded[u], (use + 1) * 16)
                    for t in range(TT):
                        wait(dve, summed, 2 * TT + n * TT + t + 1)
                        dve.tensor_tensor(y[:, u, t, :], acc[:, t, :], y[:, u, t, :], ALU.add).then_inc(y_done, 1)
                    wait(dve, y_done, n * TT + TT)
                    ln.dve_stats(dve, y[:, u], n)
                    if norm_rows is not None:
                        wait(dve, shifted, n)
                    ln.dve_z(dve, y[:, u], n)
                over_chunks(dve, body)

            @block.tensor
            def _(pe):
                pe.sem_inc(summed, 2 * TT)
                if w is not None:
                    pe.wait_ge(weights.lo_made, len(w))

                def body(n, u, use):
                    if w is not None:
                        x.pe_ready(pe, n)
                    else:
                        wait(pe, att_loaded[u], (use + 1) * 16)
                    for t in range(TT):
                        cols = slice(t * P, t * P + P)
                        wait(pe, y_done, (n - 1) * TT + t + 1)
                        for kt in range(KT):
                            if w is not None:
                                last = mm3(pe, acc[:, t, :], *x.halves(u, kt, cols), *weights.halves(kt),
                                           start=(kt == 0), stop=(kt == KT - 1))
                            else:
                                last = pe.transpose(acc[:, t, kt * P:kt * P + P], att[:, u, kt, cols],
                                                    c["ident"][:, :])
                        last.then_inc(summed, 1)
                        if t == 1 and not_first(n):
                            ln.pe_turn(pe, n - 1)
                over_chunks(pe, body)
                ln.pe_turn(pe, NCH - 1)
        st.close()



def stage_qkv(nc, tag, c, x_t, w, bias_cols, v_row, qk_out, v_out):
    with ExitStack() as ctx:
        st = Stage(nc, tag, ctx)
        tiles = 3 * KT
        done = st.sem("done")
        x = SplitInput(st, x_t, 2, lambda eng, n: wait(eng, done, n * tiles + tiles))
        weights = Weights(st, w)
        acc = st.psum("acc", [P, 4, BANK])
        hi = st.sb("hi", [P, 2, 2, KT, CH], F32R)
        lo = st.sb("lo", [P, 2, 2, KT, CH], F32R)
        v = st.sb("v", [P, TT, D])
        row = st.sb("row", [P, D])
        row_loaded = st.sem("row_loaded")
        hi_out = st.sem("hi_out")
        lo_out = st.sem("lo_out")
        v_done = st.sem("v_done")
        qk_stored = [[st.sem(f"qk_stored{i}{k}") for k in range(4)] for i in range(2)]
        v_stored = st.sem("v_stored")
        with nc.Block() as block:
            @block.sync
            def _(sp):
                sp.dma_start(row[:, :], v_row).then_inc(row_loaded, 16)
                weights.sp_load(sp)
                x.sp_load(sp, 0)

                def body(n, u, use):
                    if not_last(n):
                        x.sp_load(sp, n + 1)
                    wait(sp, lo_out, n * 8 + 8)
                    for kind in range(4):
                        tile = (hi, lo)[kind % 2]
                        sp.dma_start(qk_out[kind][:, :, bass.ds(n * CH, CH)],
                                     raw32(tile[:, u, kind // 2])).then_inc(qk_stored[u][kind], 16)
                    wait(sp, v_done, n * TT + TT)
                    sp.dma_start(v_out[:, bass.ds(n * TT, TT), :], v[:, :, :]).then_inc(v_stored, 16)
                over_chunks(sp, body)
                for s in qk_stored[0] + qk_stored[1]:
                    sp.wait_ge(s, NCH // 2 * 16)
                sp.wait_ge(v_stored, NCH * 16)

            @block.gpsimd
            def _(pool):
                x.lo_credit(pool)
                x.make_lo(pool, 0, 0)

                def body(n, u, use):
                    if not_last(n):
                        x.make_lo(pool, n + 1, 1 - u)
                over_chunks(pool, body)

            @block.scalar
            def _(act):
                weights.make_hi(act, act.copy)
                x.make_hi(act, act.copy, 0, 0)

                def body(n, u, use):
                    if not_last(n):
                        x.make_hi(act, act.copy, n + 1, 1 - u)
                    for f in range(8):
                        if f % KT == 0:
                            wait(act, qk_stored[u][2 * (f // KT)], use * 16)
                        wait(act, done, 2 * tiles + n * tiles + f + 1)
                        act.activation(hi[:, u, f // KT, f % KT, :], acc[:, f % 4, :], ACT.Identity,
                                       bias=bias_cols[:, f:f + 1]).then_inc(hi_out, 1)
                over_chunks(act, body)

            @block.vector
            def _(dve):
                weights.make_lo(dve)
                dve.wait_ge(row_loaded, 16)

                def body(n, u, use):
                    for f in range(8):
                        if f % KT == 0:
                            wait(dve, qk_stored[u][2 * (f // KT) + 1], use * 16)
                        wait(dve, hi_out, n * 8 + f + 1)
                        dve.scalar_tensor_tensor(out=lo[:, u, f // KT, f % KT, :], in0=acc[:, f % 4, :],
                                                 scalar=bias_cols[:, f:f + 1],
                                                 in1=raw32(hi[:, u, f // KT, f % KT, :]),
                                                 op0=ALU.add, op1=ALU.subtract).then_inc(lo_out, 1)
                    wait(dve, v_stored, n * 16)
                    for t in range(TT):
                        wait(dve, done, 2 * tiles + n * tiles + 8 + t + 1)
                        dve.tensor_tensor(v[:, t, :], acc[:, t, :], row[:, :], ALU.add).then_inc(v_done, 1)
                over_chunks(dve, body)

            @block.tensor
            def _(pe):
                pe.sem_inc(done, 2 * tiles)
                pe.wait_ge(weights.lo_made, len(w))

                def body(n, u, use):
                    x.pe_ready(pe, n)
                    for f in range(8):
                        if f < 4:
                            wait(pe, v_done, (n - 1) * TT + f + 1)
                        else:
                            wait(pe, lo_out, n * 8 + f - 3)
                        for kt in range(KT):
                            cols = slice((f % KT) * P, (f % KT) * P + P)
                            last = mm3(pe, acc[:, f % 4, :], *weights.halves((f // KT) * KT + kt, cols),
                                       *x.halves(u, kt, slice(0, CH)), start=(kt == 0), stop=(kt == KT - 1))
                        last.then_inc(done, 1)
                    for t in range(TT):
                        wait(pe, lo_out, n * 8 + 5 + t)
                        for kt in range(KT):
                            last = mm3(pe, acc[:, t, :], *x.halves(u, kt, slice(t * P, t * P + P)),
                                       *weights.halves(2 * KT + kt), start=(kt == 0), stop=(kt == KT - 1))
                        last.then_inc(done, 1)
                over_chunks(pe, body)
        st.close()



def stage_cross(nc, tag, c, x_t, wq, q_bias, ctx_t, wk, k_bias, wv, v_bias, att_out, causal):
    with ExitStack() as outer:
        st = Stage(nc, tag, outer)
        k_hi = st.sb("k_hi", [P, B, G, KEYS], F32R)
        k_lo = st.sb("k_lo", [P, B, G, KEYS], F32R)
        v = st.sb("v", [SK, B, D])
        mask = st.sb("mask", [P, NCH, SK], BF16)

        with ExitStack() as ctx:
            cs = Stage(nc, f"{tag}_ctx", ctx)
            ctx_sb = cs.sb("ctx", [P, KT, B * SK])
            wk_sb = cs.sb("wk", [P, KT, D])
            wv_sb = cs.sb("wv", [P, KT, D])
            mask32 = cs.sb("mask32", [P, SK])
            kp = cs.psum("kp", [P, G, BANK])
            vp = cs.psum("vp", [P, B, BANK])
            loaded = cs.sem("loaded")
            zeroed = cs.sem("zeroed")
            mask_made = cs.sem("mask_made")
            k_summed = cs.sem("k_summed")
            v_summed = cs.sem("v_summed")
            hi_done = cs.sem("hi_done")
            lo_done = cs.sem("lo_done")
            v_done = cs.sem("v_done")
            with nc.Block() as block:
                @block.sync
                def _(sp):
                    sp.dma_start(ctx_sb[:, :, :], ctx_t).then_inc(loaded, 16)
                    for kt in range(KT):
                        sp.dma_start(wk_sb[:, kt, :], wk[kt]).then_inc(loaded, 16)
                        sp.dma_start(wv_sb[:, kt, :], wv[kt]).then_inc(loaded, 16)

                @block.gpsimd
                def _(pool):
                    pool.memset(mask[:, :, :], 0.0).then_inc(mask_made, 1)
                    if causal:
                        pool.memset(mask32[:, :], 0.0).then_inc(mask_made, 1)
                        pool.wait_ge(mask_made, 2)
                        pool.affine_select(out=mask32[:, :], in_=mask32[:, :], compare_op=ALU.is_ge,
                                           fill=MASKED, base=0, pattern=[[-1, SK]],
                                           channel_multiplier=1).then_inc(mask_made, 1)
                        pool.wait_ge(mask_made, 3)
                        for b in range(B):
                            pool.tensor_copy(mask[:, b * CPB, :], mask32[:, :]).then_inc(mask_made, 1)

                @block.vector
                def _(dve):
                    dve.memset(raw32(k_hi[:, :, :, :]), 0.0).then_inc(zeroed, 1)
                    dve.memset(raw32(k_lo[:, :, :, :]), 0.0).then_inc(zeroed, 1)
                    for g in range(G):
                        for h in range(HG):
                            part = slice(h * DH, h * DH + DH)
                            dve.wait_ge(hi_done, g * HG + h + 1)
                            keys = slice(h * SK, h * SK + SK)
                            dve.scalar_tensor_tensor(
                                out=k_lo[part, :, g, keys],
                                in0=kp[part, g, 0:B * SK].rearrange("p (b k) -> p b k", b=B),
                                scalar=k_bias[part, g:g + 1], in1=raw32(k_hi[part, :, g, keys]),
                                op0=ALU.add, op1=ALU.subtract).then_inc(lo_done, 1)
                    for b in range(B):
                        dve.wait_ge(v_summed, b + 1)
                        dve.tensor_copy(v[:, b, :], vp[0:SK, b, :]).then_inc(v_done, 1)

                @block.scalar
                def _(act):
                    act.wait_ge(zeroed, 2)
                    for g in range(G):
                        act.wait_ge(k_summed, g + 1)
                        for h in range(HG):
                            part = slice(h * DH, h * DH + DH)
                            act.activation(k_hi[part, :, g, h * SK:h * SK + SK],
                                           kp[part, g, 0:B * SK].rearrange("p (b k) -> p b k", b=B),
                                           ACT.Identity, bias=k_bias[part, g:g + 1]).then_inc(hi_done, 1)

                @block.tensor
                def _(pe):
                    pe.wait_ge(loaded, 16 * (1 + 2 * KT))
                    for g in range(G):
                        for kt in range(KT):
                            last = pe.matmul(kp[:, g, 0:B * SK], wk_sb[:, kt, g * P:g * P + P], ctx_sb[:, kt, :],
                                             start=(kt == 0), stop=(kt == KT - 1))
                        last.then_inc(k_summed, 1)
                    for b in range(B):
                        for kt in range(KT):
                            last = pe.matmul(vp[0:SK, b, :], ctx_sb[:, kt, b * SK:b * SK + SK], wv_sb[:, kt, :],
                                             start=(kt == 0), stop=(kt == KT - 1))
                        last.then_inc(v_summed, 1)
            cs.close()

        q_done = st.sem("q_done")
        scored = st.sem("scored")
        x = SplitInput(st, x_t, 2, lambda eng, n: wait(eng, scored, n * TT + TT))
        weights = Weights(st, wq)
        q_hi = st.sb("q_hi", [P, 2, G, CH], F32R)
        q_lo = st.sb("q_lo", [P, 2, G, CH], F32R)
        e = st.sb("e", [P, 2, H, SK])
        probs = st.sb("probs", [P, 2, H, SK])
        probs_t = st.sb("probs_t", [SK, H, P])
        v_now = st.sb("v_now", [SK, 2, D])
        biggest = st.sb("biggest", [P, H])
        total = st.sb("total", [P, H])
        inverse = st.sb("inverse", [P, 2, H])
        att = st.sb("att", [P, 2, G, CH])
        scores = st.psum("scores", [P, G, BANK])
        qp = st.psum("qp", [P, BANK])
        turned_p = st.psum("turned_p", [SK, 2, BANK])
        att_p = st.psum("att_p", [P, BANK])
        q_hi_done = st.sem("q_hi_done")
        q_lo_done = st.sem("q_lo_done")
        max_done = st.sem("max_done")
        shifted = st.sem("shifted")
        exp_done = st.sem("exp_done")
        sum_done = st.sem("sum_done")
        inverse_done = st.sem("inverse_done")
        probs_done = st.sem("probs_done")
        turned = st.sem("turned")
        left_act = st.sem("left_act")
        left_dve = st.sem("left_dve")
        v_ready = st.sem("v_ready")
        summed = st.sem("summed")
        att_done = st.sem("att_done")
        att_stored = [st.sem(f"att_stored{i}") for i in range(2)]
        last_m = NCH * TT - 1

        def steps(body):
            def chunk(n, u, use):
                for t in range(TT):
                    body(n * TT + t, n, t, u, use)
            return chunk

        def ago(m, n, t, u, lag):
            if isinstance(m, int) and m < lag:
                return None
            return (n, t - lag, u) if t >= lag else (n - 1, t - lag + TT, 1 - u)

        with nc.Block() as block:
            @block.sync
            def _(sp):
                weights.sp_load(sp)
                x.sp_load(sp, 0)
                x.sp_load(sp, 1)

                def body(n, u, use):
                    if not (isinstance(n, int) and n >= NCH - 2):
                        x.sp_load(sp, n + 2)
                    wait(sp, att_done, n * TT + TT)
                    sp.dma_start(att_out[:, :, bass.ds(n * CH, CH)], att[:, u]).then_inc(att_stored[u], 16)
                body(0, 0, 0)
                with sp.Fori(0, (NCH - 4) // 2) as i:
                    body(2 * i + 1, 1, i)
                    body(2 * i + 2, 0, i + 1)
                for n in range(NCH - 3, NCH):
                    body(n, n % 2, n // 2)
                for s in att_stored:
                    sp.wait_ge(s, NCH // 2 * 16)

            @block.gpsimd
            def _(pool):
                x.lo_credit(pool)
                pool.sem_inc(probs_done, 2)
                x.make_lo(pool, 0, 0)

                def body(m, n, t, u, use):
                    if t == 0:
                        if not_last(n):
                            x.make_lo(pool, n + 1, 1 - u)
                        wait(pool, summed, n * TT + TT)
                        pool.tensor_copy(v_now[:, u, :],
                                         v[:, bass.ds(n // CPB, 1), :]).then_inc(v_ready, 1)
                    past = ago(m, n, t, u, 1)
                    if past:
                        normalize(m - 1, past)

                def normalize(m, at):
                    slot = at[1] % 2
                    wait(pool, inverse_done, m + 1)
                    wait(pool, turned, (m - 1) * G)
                    pool.tensor_tensor(probs[:, slot], e[:, slot],
                                       inverse[:, slot, :].unsqueeze(2).to_broadcast([P, H, SK]),
                                       ALU.mult).then_inc(probs_done, 1)
                over_chunks(pool, steps(body))
                normalize(last_m, (NCH - 1, TT - 1, 1))

            @block.scalar
            def _(act):
                weights.make_hi(act, act.copy)
                x.make_hi(act, act.copy, 0, 0)

                def leave(m):
                    for i, g in enumerate((0, 1, 2)):
                        wait(act, turned, m * G + g + 1)
                        if g == 0:
                            wait(act, summed, 2 * TT + m)
                        act.copy(probs_t[:, g * HG:g * HG + HG, :],
                                 turned_p[:, g % 2, :]).then_inc(left_act, 1)

                def q_out(k, n, g, u):
                    wait(act, q_done, k + 1)
                    act.activation(q_hi[:, u, g, :], qp[:, :], ACT.Identity,
                                   bias=q_bias[:, g:g + 1]).then_inc(q_hi_done, 1)

                for g in range(G):
                    q_out(g, 0, g, 0)

                def body(m, n, t, u, use):
                    if t == 0 and not_last(n):
                        x.make_hi(act, act.copy, n + 1, 1 - u)
                    wait(act, shifted, m + 1)
                    act.activation(e[:, t % 2], e[:, t % 2], ACT.Exp, scale=SCALE).then_inc(exp_done, 1)
                    if not_last(n):
                        q_out((n + 1) * G + t, n + 1, t, 1 - u)
                    if ago(m, n, t, u, 1):
                        leave(m - 1)
                over_chunks(act, steps(body))
                leave(last_m)

            @block.vector
            def _(dve):
                weights.make_lo(dve)

                def sums(m, slot):
                    wait(dve, exp_done, m + 1)
                    dve.tensor_reduce(total[:, :], e[:, slot], AX_X, ALU.add).then_inc(sum_done, 1)
                    wait(dve, sum_done, m + 1)
                    dve.reciprocal(inverse[:, slot, :], total[:, :]).then_inc(inverse_done, 1)

                def att_leave(m, at):
                    n, t, u = at
                    if t == 0 and not (isinstance(n, int) and n < 2):
                        wait(dve, att_stored[u], 16 * (n // 2))
                    wait(dve, summed, 2 * TT + m + 1)
                    dve.tensor_tensor(att[:, u, :, t * P:t * P + P], att_p[:, :].rearrange("p (g q) -> p g q", g=G),
                                      v_bias.unsqueeze(2).to_broadcast([P, G, P]), ALU.add).then_inc(att_done, 1)

                def q_out(k, n, g, u):
                    wait(dve, q_hi_done, k + 1)
                    dve.scalar_tensor_tensor(out=q_lo[:, u, g, :], in0=qp[:, :], scalar=q_bias[:, g:g + 1],
                                             in1=raw32(q_hi[:, u, g, :]), op0=ALU.add,
                                             op1=ALU.subtract).then_inc(q_lo_done, 1)

                def leave(m):
                    wait(dve, turned, m * G + G)
                    dve.tensor_copy(probs_t[:, 3 * HG:H, :], turned_p[:, 1, :]).then_inc(left_dve, 1)

                for g in range(G):
                    q_out(g, 0, g, 0)

                def body(m, n, t, u, use):
                    past, older = ago(m, n, t, u, 1), ago(m, n, t, u, 2)
                    if past:
                        sums(m - 1, past[1] % 2)
                    view = scores[:, :, 0:KEYS].rearrange("p g (h k) -> p g h k", h=HG)
                    wait(dve, scored, 2 * TT + m + 1)
                    dve.tensor_reduce(biggest[:, :].rearrange("p (g h) -> p g h", g=G), view, AX_X,
                                      ALU.max).then_inc(max_done, 1)
                    wait(dve, max_done, m + 1)
                    wait(dve, probs_done, m + 1)
                    for g in range(G):
                        hs = slice(g * HG, g * HG + HG)
                        last = dve.tensor_tensor(e[:, t % 2, hs, :],
                                                 scores[:, g, 0:KEYS].rearrange("p (h k) -> p h k", h=HG),
                                                 biggest[:, hs].unsqueeze(2).to_broadcast([P, HG, SK]),
                                                 ALU.subtract)
                    last.then_inc(shifted, 1)
                    if older:
                        att_leave(m - 2, older)
                    if not_last(n):
                        q_out((n + 1) * G + t, n + 1, t, 1 - u)
                    if past:
                        leave(m - 1)
                over_chunks(dve, steps(body))
                sums(last_m, 1)
                att_leave(last_m - 1, (NCH - 1, TT - 2, 1))
                leave(last_m)
                att_leave(last_m, (NCH - 1, TT - 1, 1))

            @block.tensor
            def _(pe):
                pe.sem_inc(scored, 2 * TT)
                pe.sem_inc(summed, 2 * TT)
                pe.wait_ge(weights.lo_made, len(wq))

                def project(k, n, g, u):
                    if g == 0:
                        x.pe_ready(pe, n)
                    wait(pe, q_lo_done, k)
                    for kt in range(KT):
                        last = mm3(pe, qp[:, :], *weights.halves(kt, slice(g * P, g * P + P)),
                                   *x.halves(u, kt, slice(0, CH)), start=(kt == 0), stop=(kt == KT - 1))
                    last.then_inc(q_done, 1)

                def score(m, n, t, u):
                    wait(pe, shifted, m)
                    wait(pe, q_lo_done, n * G + G)
                    cols = slice(t * P, t * P + P)
                    for g in range(G):
                        at = (slice(None), bass.ds(n // CPB, 1), g)
                        masked = causal and t == 0
                        last = mm3(pe, scores[:, g, 0:KEYS], q_hi[:, u, g, cols], q_lo[:, u, g, cols],
                                   k_hi[at], k_lo[at], start=True, stop=not masked)
                        if masked:
                            last = pe.matmul(scores[:, g, 0:KEYS], c["ident_bf"][:, :],
                                             mask[:, bass.ds(n, 1), :].to_broadcast([P, HG, SK]),
                                             start=False, stop=True)
                    last.then_inc(scored, 1)

                def turn(m, slot):
                    wait(pe, probs_done, m + 3)
                    for g in range(G):
                        if g < 2:
                            if g == 0:
                                wait(pe, left_act, 3 * m)
                            else:
                                wait(pe, left_dve, m)
                        else:
                            wait(pe, left_act, 3 * m + g - 1)
                        for h in range(HG):
                            last = pe.transpose(turned_p[:, g % 2, h * P:h * P + P],
                                                probs[:, slot, g * HG + h, :], c["ident"][:, :])
                        last.then_inc(turned, 1)

                def weigh(m, at):
                    n, t, u = at
                    wait(pe, left_act, 3 * m + 3)
                    wait(pe, left_dve, m + 1)
                    wait(pe, v_ready, n + 1)
                    wait(pe, att_done, m)
                    for g in range(G):
                        for h in range(HG):
                            head = g * HG + h
                            last = pe.matmul(att_p[h * DH:h * DH + DH, g * P:g * P + P],
                                             v_now[:, u, head * DH:head * DH + DH], probs_t[:, head, :],
                                             start=True, stop=True)
                    last.then_inc(summed, 1)

                for g in range(G):
                    project(g, 0, g, 0)

                def body(m, n, t, u, use):
                    past, older = ago(m, n, t, u, 1), ago(m, n, t, u, 2)
                    score(m, n, t, u)
                    if older:
                        weigh(m - 2, older)
                    if not_last(n):
                        project((n + 1) * G + t, n + 1, t, 1 - u)
                    if past:
                        turn(m - 1, past[1] % 2)
                over_chunks(pe, steps(body))
                weigh(last_m - 1, (NCH - 1, TT - 2, 1))
                turn(last_m, 1)
                weigh(last_m, (NCH - 1, TT - 1, 1))
        st.close()



def stage_self(nc, tag, c, qk, v_in, att_out):
    NQ = S // CH
    NW = B * G
    STACK = 3 * DH
    units = [TT * (q + 1) for q in range(NQ)]
    first_unit = [sum(units[:q]) for q in range(NQ)]
    UNITS = sum(units)

    LAG = 5
    items, rows_due = [], []
    for q in range(NQ):
        for h in range(HG):
            for t in range(TT):
                for block_ in range(q + 1):
                    items.append(("scores", q, h, t, block_))
                    if rows_due and len(items) >= rows_due[0][0]:
                        items.append(rows_due.pop(0)[1])
            rows_due.append((len(items) + LAG, ("row", q, h)))
    items += [row for _, row in rows_due]
    ITEMS = len(items)
    row_at = {(it[1], it[2]): i for i, it in enumerate(items) if it[0] == "row"}
    BEFORE = row_at[0, HG - 1] + 1
    STEADY = ITEMS * 2 // 5

    def lot(w, g):
        rest = first_unit[NQ - 1]
        done = {rest - 2: ITEMS - 2, rest: ITEMS, UNITS: ITEMS + STEADY}
        if not_first(w):
            done[0] = STEADY
        else:
            done[0] = BEFORE
            for q in range(1, NQ - 1):
                done[first_unit[q]] = row_at[q, HG - 1] + 1
        marks = sorted(done)

        def by(unit):
            at = max(m for m in marks if m <= unit)
            if at == UNITS:
                return done[UNITS]
            to = min(m for m in marks if m > unit)
            return done[at] + (done[to] - done[at]) * (unit - at) // (to - at)
        for q in range(1, NQ):
            assert by(first_unit[q]) > row_at[q, HG - 1]
        span = range(by(g), by(g + 1))
        return [i for i in span if i < ITEMS or not_last(w, NW)]

    def parts(w, g):
        todo = lot(w, g)
        return [todo[len(todo) * k // 4:len(todo) * (k + 1) // 4] for k in range(4)]

    with ExitStack() as ctx:
        st = Stage(nc, tag, ctx)
        ks = st.sb("ks", [P, 2, HG, S], F32R)
        qs = st.sb("qs", [P, 2, HG, S], F32R)
        v = st.sb("v", [P, 2, S // P, P])
        pt = st.sb("pt", [P, 2, HG, CH])
        diag = st.sb("diag", [P, HG, CH], F32R)
        ones_r = st.sb("ones_r", [P, P], F32R)
        ones = st.sb("ones", [P, DH])
        mask32 = st.sb("mask32", [P, P])
        mask_q = st.sb("mask_q", [P, P], BF16)
        mask_k = st.sb("mask_k", [P, P], BF16)
        part_max = st.sb("part_max", [P, HG, TT, NQ])
        neg_max = st.sb("neg_max", [P, HG, TT])
        weighted = st.sb("weighted", [P, CH])
        total = st.sb("total", [P, CH])
        att = st.sb("att", [P, 2, CH])
        sc = st.psum("sc", [P, 2, 2, BANK])
        mp = st.psum("mp", [P, 2, BANK])
        out = st.psum("out", [P, BANK])
        den = st.psum("den", [P, BANK])

        const_made = st.sem("const_made")
        ready = st.sem("ready")
        k_loaded = [st.sem(f"k_loaded{i}") for i in range(2)]
        item_done = st.sem("item_done")
        item_read = st.sem("item_read")
        max_done = st.sem("max_done")
        diag_done = st.sem("diag_done")
        scored = st.sem("scored")
        exp_done = st.sem("exp_done")
        unit_done = st.sem("unit_done")
        left = st.sem("left")
        inverse_done = st.sem("inverse_done")
        att_done = st.sem("att_done")
        att_stored = [st.sem(f"att_stored{i}") for i in range(2)]

        def over_pairs(eng, body):
            over_chunks(eng, body, NW)

        def chunk_number(w, q):
            return w * NQ + q

        def unit_number(w, q, k):
            return w * UNITS + first_unit[q] + k

        def before(w, u, q, k):
            if k > 0:
                return w, u, q, k - 1
            if q > 0:
                return w, u, q - 1, units[q - 1] - 1
            return (w - 1, 1 - u, NQ - 1, units[NQ - 1] - 1) if not_first(w) else None

        def width_of(q, t, block_):
            return min(CH, (q * TT + t + 1) * P - block_ * CH)

        with nc.Block() as block:
            @block.sync
            def _(sp):
                def load(w, u):
                    wait(sp, unit_done, (w - 1) * UNITS)
                    b, g = w // G, w % G
                    toks = bass.ds(b * S, S)

                    for dst, kinds in ((ks, (2, 2, 3)), (qs, (0, 1, 0))):
                        for part, kind in enumerate(kinds):
                            src = qk[kind][:, bass.ds(g, 1), toks].rearrange("(h r) o t -> r (h o) t", r=DH)
                            sp.dma_start(raw32(dst[part * DH:part * DH + DH, u]), src).then_inc(k_loaded[u], 16)
                    sp.dma_start(v[:, u], v_in[:, bass.ds(b * (S // P), S // P),
                                               bass.ds(g * P, P)]).then_inc(k_loaded[u], 16)
                load(0, 0)

                def body(w, u, use):
                    if not_last(w, NW):
                        load(w + 1, 1 - u)
                    b, g = w // G, w % G
                    for q in range(NQ):
                        wait(sp, att_done, chunk_number(w, q) + 1)
                        sp.dma_start(att_out[:, bass.ds(g, 1), bass.ds(b * S + q * CH, CH)],
                                     att[:, q % 2, :].unsqueeze(1)).then_inc(att_stored[q % 2], 16)
                over_pairs(sp, body)
                for s in att_stored:
                    sp.wait_ge(s, NW * NQ // 2 * 16)

            @block.gpsimd
            def _(pool):
                pool.memset(mask32[:, :], 0.0).then_inc(const_made, 1)
                pool.wait_ge(const_made, 1)
                pool.affine_select(out=mask32[:, :], in_=mask32[:, :], compare_op=ALU.is_ge, fill=MASKED,
                                   base=0, pattern=[[-1, P]], channel_multiplier=1).then_inc(const_made, 1)
                pool.wait_ge(const_made, 2)
                pool.tensor_copy(mask_q[:, :], mask32[:, :]).then_inc(const_made, 1)
                pool.wait_ge(const_made, 3)
                pool.memset(mask32[:, :], 0.0).then_inc(const_made, 1)
                pool.wait_ge(const_made, 4)
                pool.affine_select(out=mask32[:, :], in_=mask32[:, :], compare_op=ALU.is_ge, fill=MASKED,
                                   base=0, pattern=[[1, P]], channel_multiplier=-1).then_inc(const_made, 1)
                pool.wait_ge(const_made, 5)
                pool.tensor_copy(mask_k[:, :], mask32[:, :]).then_inc(const_made, 1)

                def body(w, u, use):
                    for q in range(NQ):
                        for h in range(HG):
                            if q > 0:
                                wait(pool, item_done, w * ITEMS + row_at[q - 1, h] + 1)
                            elif not_first(w):
                                wait(pool, item_done, (w - 1) * ITEMS + row_at[NQ - 1, h] + 1)
                            wait(pool, max_done, chunk_number(w, q) * HG + h + 1)
                            pool.tensor_tensor(diag[:, h, :].rearrange("p (t q) -> p t q", t=TT),
                                               c["ident"][:, :].unsqueeze(1).to_broadcast([P, TT, P]),
                                               neg_max[:, h, :].unsqueeze(2).to_broadcast([P, TT, P]),
                                               ALU.mult).then_inc(diag_done, 1)
                over_pairs(pool, body)

            @block.vector
            def _(dve):
                for slot in range(2):
                    dve.memset(raw32(ks[STACK:STACK + 1, slot]), 1.0).then_inc(ready, 1)
                dve.memset(raw32(ones_r[:, :]), 1.0).then_inc(ready, 1)
                dve.memset(ones[:, :], 1.0).then_inc(ready, 1)

                def read(w, u, base, lot_):
                    for i in lot_:
                        kind, q, h, *at = items[i]
                        wait(dve, item_done, base + i + 1)
                        if kind == "row":
                            dve.tensor_copy(qs[STACK:STACK + 1, u, h, q * CH:q * CH + CH],
                                            mp[STACK:STACK + 1, i % 2, :]).then_inc(item_read, 1)
                            continue
                        t, block_ = at
                        dve.tensor_reduce(part_max[:, h, t, block_:block_ + 1],
                                          mp[:, i % 2, 0:width_of(q, t, block_)],
                                          AX_X, ALU.max).then_inc(item_read, 1)
                        if (t, block_) == (TT - 1, q):
                            wait(dve, diag_done, (chunk_number(w, q) - 1) * HG + h + 1)
                            wait(dve, item_read, base + i + 1)
                            dve.tensor_reduce(neg_max[:, h, :], part_max[:, h, :, 0:q + 1], AX_X, ALU.max,
                                              negate=True).then_inc(max_done, 1)
                read(0, 0, 0, range(BEFORE))

                def invert(w, q, t):
                    wait(dve, left, chunk_number(w, q) * 2 + 2)
                    cols = slice(t * P, t * P + P)
                    dve.reciprocal(total[:, cols], total[:, cols]).then_inc(inverse_done, 1)

                def leave(w, q):
                    wait(dve, att_stored[q % 2], (w * 2 + q // 2) * 16)
                    wait(dve, inverse_done, (chunk_number(w, q) + 1) * TT)
                    dve.tensor_tensor(att[:, q % 2, :], weighted[:, :], total[:, :], ALU.mult).then_inc(att_done, 1)

                def body(w, u, use):
                    for q in range(NQ):
                        for k in range(units[q]):
                            past = before(w, u, q, 0)
                            for part, lot_ in enumerate(parts(w, first_unit[q] + k)):
                                for i in lot_:
                                    if i < ITEMS:
                                        read(w, u, w * ITEMS, [i])
                                    else:
                                        read(w + 1, 1 - u, (w + 1) * ITEMS, [i - ITEMS])
                                if k == 1 and past:
                                    invert(past[0], past[2], part)
                            if k == 1 and past:
                                leave(past[0], past[2])
                over_pairs(dve, body)
                for t in range(TT):
                    invert(NW - 1, NQ - 1, t)
                leave(NW - 1, NQ - 1)

            @block.scalar
            def _(act):
                def leave(w, q):
                    wait(act, unit_done, unit_number(w, q, units[q]))
                    wait(act, att_done, chunk_number(w, q))
                    act.copy(weighted[:, :], out[:, :]).then_inc(left, 1)
                    act.copy(total[:, :], den[:, :]).then_inc(left, 1)

                def body(w, u, use):
                    for q in range(NQ):
                        for k in range(units[q]):
                            number = unit_number(w, q, k)
                            start = max(0, k - q * TT) * P
                            for pair in range(2):
                                wait(act, unit_done, number - 1)
                                wait(act, scored, number * 2 + pair + 1)
                                act.activation(pt[:, k % 2, 2 * pair:2 * pair + 2, start:CH],
                                               sc[:, pair, :, start:CH], ACT.Exp,
                                               scale=SCALE).then_inc(exp_done, 1)
                            past = before(w, u, q, k)
                            if k == 0 and past:
                                leave(past[0], past[2])
                over_pairs(act, body)
                leave(NW - 1, NQ - 1)

            @block.tensor
            def _(pe):
                def run_items(w, u, base, lot_):
                    for i in lot_:
                        kind, q, h, *at = items[i]
                        if kind == "row":
                            wait(pe, diag_done, chunk_number(w, q) * HG + h + 1)
                            wait(pe, item_read, base + i - 1)
                            pe.matmul(mp[:, i % 2, :], ones_r[:, :], diag[:, h, :],
                                      start=True, stop=True).then_inc(item_done, 1)
                            continue
                        t, block_ = at
                        width = width_of(q, t, block_)
                        tile = (q * TT + t) * P
                        wait(pe, item_read, base + i - 1)
                        last = pe.matmul(mp[:, i % 2, 0:width], qs[0:STACK, u, h, tile:tile + P],
                                         ks[0:STACK, u, h, block_ * CH:block_ * CH + width],
                                         start=True, stop=block_ < q)
                        if block_ == q:
                            last = pe.matmul(mp[:, i % 2, width - P:width], c["ident_bf"][:, :], mask_q[:, :],
                                             start=False, stop=True)
                        last.then_inc(item_done, 1)

                def score(w, u, q, k, pair):
                    number = unit_number(w, q, k)
                    start = max(0, k - q * TT) * P
                    if k == 0:
                        wait(pe, item_read, w * ITEMS + row_at[q, 2 * pair + 1] + 1)
                    wait(pe, exp_done, (number - 1) * 2 + pair + 1)
                    for i in range(2):
                        h = 2 * pair + i
                        diagonal = k >= q * TT
                        last = pe.matmul(sc[:, pair, i, start:CH],
                                         ks[0:STACK + 1, u, h, k * P:k * P + P],
                                         qs[0:STACK + 1, u, h, q * CH + start:q * CH + CH],
                                         start=True, stop=not diagonal)
                        if diagonal:
                            last = pe.matmul(sc[:, pair, i, start:start + P], c["ident_bf"][:, :],
                                             mask_k[:, :], start=False, stop=True)
                    last.then_inc(scored, 1)

                def weigh(w, u, q, k):
                    number = unit_number(w, q, k)
                    start = max(0, k - q * TT) * P
                    if k == 0:
                        wait(pe, left, chunk_number(w, q) * 2)
                    wait(pe, exp_done, number * 2 + 2)
                    for h in range(HG):
                        part = slice(h * DH, h * DH + DH)
                        pe.matmul(out[part, start:CH], v[:, u, k, part], pt[:, k % 2, h, start:CH],
                                  start=(k == 0), stop=(k == units[q] - 1))

                def add_up(w, u, q, k):
                    start = max(0, k - q * TT) * P
                    for h in range(HG):
                        part = slice(h * DH, h * DH + DH)
                        last = pe.matmul(den[part, start:CH], ones[:, :], pt[:, k % 2, h, start:CH],
                                         start=(k == 0), stop=(k == units[q] - 1))
                    last.then_inc(unit_done, 1)

                pe.wait_ge(ready, 4)
                pe.wait_ge(const_made, 6)
                pe.wait_ge(k_loaded[0], 7 * 16)
                run_items(0, 0, 0, range(BEFORE))

                def body(w, u, use):
                    for q in range(NQ):
                        for k in range(units[q]):
                            past = before(w, u, q, k)
                            for part, lot_ in enumerate(parts(w, first_unit[q] + k)):
                                if part < 2:
                                    score(w, u, q, k, part)
                                elif past and part == 2:
                                    weigh(*past)
                                elif past:
                                    add_up(*past)
                                for i in lot_:
                                    if i == ITEMS:
                                        wait(pe, k_loaded[1 - u], (use + u + 1) * 7 * 16)
                                    if i < ITEMS:
                                        run_items(w, u, w * ITEMS, [i])
                                    else:
                                        run_items(w + 1, 1 - u, (w + 1) * ITEMS, [i - ITEMS])
                over_pairs(pe, body)
                weigh(NW - 1, 1, NQ - 1, units[NQ - 1] - 1)
                add_up(NW - 1, 1, NQ - 1, units[NQ - 1] - 1)
        st.close()



COLUMNS = {}
for _name, _n in (("L0_bq", 4), ("L0_bk", 4), ("L0_bv", 4), ("L0_ln_g", 4), ("L0_ln_b", 4), ("L0_b1", FT),
                  ("L1_ln1_g", 4), ("L1_ln1_b", 4), ("L1_qkv_b", 12), ("L1_ln2_g", 4), ("L1_ln2_b", 4),
                  ("L1_q_b", 4), ("L1_k_b", 4), ("L1_v_b", 4), ("L1_ln3_g", 4), ("L1_ln3_b", 4), ("L1_fc_b", FT)):
    COLUMNS[_name] = (sum(n for _, n in COLUMNS.values()), _n)
ROWS = ("L0_ln_g", "L0_ln_b", "L0_b2", "L1_v_b", "L1_attn_proj_b", "L1_ca_proj_b", "L1_proj_b")


def build(nc, d):
    def features(ap):
        return ap.rearrange("(k p) t -> p k t", p=P)

    def tokens(ap):
        return ap.rearrange("(n p) d -> p n d", p=P)

    def scratch(name, shape):
        return nc.dram_tensor(name, shape, F32, kind="Internal").ap()

    def pieces(name):
        return [d[name][k] for k in range(d[name].shape[0])]

    def row(name):
        r = ROWS.index(name)
        return d["rows"][r:r + 1, :].to_broadcast([P, D])

    att_t = features(scratch("att_t", (D, TOK)))
    att2_t = features(scratch("att2_t", (D, TOK)))
    norm_t = features(scratch("norm_t", (D, TOK)))
    norm2_t = features(scratch("norm2_t", (D, TOK)))
    y_a = tokens(scratch("y_a", (TOK, D)))
    y_b = tokens(scratch("y_b", (TOK, D)))
    v_all = tokens(scratch("v_all", (TOK, D)))
    qk = [features(scratch(f"qk{k}", (D, TOK))) for k in range(4)]

    with ExitStack() as ctx:
        c = {}
        build_constants(nc, ctx, c)
        load_columns(nc, ctx, d, c)

        def col(name):
            first, n = COLUMNS[name]
            return c["cols"][:, first:first + n]

        stage_cross(nc, "ca0", c, features(d["x_t"]), pieces("L0_wq"), col("L0_bq"), features(d["ctx_t"]),
                    pieces("L0_wk"), col("L0_bk"), pieces("L0_wv"), col("L0_bv"), att_t, causal=True)
        stage_merge(nc, "ln0", c, att_t, tokens(d["x"]), (col("L0_ln_g"), col("L0_ln_b"), norm_t), y_a,
                    norm_rows=(row("L0_ln_g"), row("L0_ln_b")))
        stage_ff(nc, "ff0", c, norm_t, y_a, pieces("L0_w1"), pieces("L0_w2"), col("L0_b1"), row("L0_b2"), y_b,
                 (col("L1_ln1_g"), col("L1_ln1_b"), norm2_t))
        stage_qkv(nc, "qkv", c, norm2_t, pieces("L1_wqkv"), col("L1_qkv_b"), row("L1_v_b"), qk, v_all)
        stage_self(nc, "sa", c, qk, v_all, att2_t)
        stage_merge(nc, "pr1", c, att2_t, y_b, (col("L1_ln2_g"), col("L1_ln2_b"), norm_t), y_a,
                    w=pieces("L1_wproj"), bias_row=row("L1_attn_proj_b"))
        stage_cross(nc, "ca1", c, norm_t, pieces("L1_wq"), col("L1_q_b"), features(d["ctx_t"]),
                    pieces("L1_wk"), col("L1_k_b"), pieces("L1_wv"), col("L1_v_b"), att_t, causal=False)
        stage_merge(nc, "pr2", c, att_t, y_a, (col("L1_ln3_g"), col("L1_ln3_b"), norm2_t), y_b,
                    w=pieces("L1_wcaproj"), bias_row=row("L1_ca_proj_b"))
        stage_ff(nc, "ff1", c, norm2_t, y_b, pieces("L1_w1"), pieces("L1_w2"), col("L1_fc_b"),
                 row("L1_proj_b"), tokens(d["out"]))


def lay_out(inputs):
    import numpy as np
    a = {k: np.asarray(v) for k, v in inputs.items()}

    def by_input(w):
        return np.ascontiguousarray(w.T.reshape(w.shape[1] // P, P, w.shape[0]))

    def up(w):
        return np.ascontiguousarray(w.T.reshape(KT, P, FT, P).transpose(2, 1, 0, 3).reshape(FT, P, D))

    def column(v):
        return v.reshape(-1, P).T

    cols = {"L0_bq": "L0_xattn_bq", "L0_bk": "L0_xattn_bk", "L0_bv": "L0_xattn_bv", "L0_ln_g": "L0_xattn_ln_g",
            "L0_ln_b": "L0_xattn_ln_b", "L0_b1": "L0_xattn_b1", "L1_ln1_g": "L1_xattn_ln1_g",
            "L1_ln1_b": "L1_xattn_ln1_b", "L1_qkv_b": "L1_xattn_attn_qkv_b", "L1_ln2_g": "L1_xattn_ln2_g",
            "L1_ln2_b": "L1_xattn_ln2_b", "L1_q_b": "L1_xattn_q_b", "L1_k_b": "L1_xattn_k_b",
            "L1_v_b": "L1_xattn_v_b", "L1_ln3_g": "L1_xattn_ln3_g", "L1_ln3_b": "L1_xattn_ln3_b",
            "L1_fc_b": "L1_xattn_fc_b"}
    rows = {"L0_ln_g": a["L0_xattn_ln_g"], "L0_ln_b": a["L0_xattn_ln_b"], "L0_b2": a["L0_xattn_b2"],
            "L1_v_b": a["L1_xattn_attn_qkv_b"][2 * D:], "L1_attn_proj_b": a["L1_xattn_attn_proj_b"],
            "L1_ca_proj_b": a["L1_xattn_ca_proj_b"], "L1_proj_b": a["L1_xattn_proj_b"]}
    x = a["x"].reshape(TOK, D)
    qkv = a["L1_xattn_attn_qkv_w"]
    return {
        "x": np.ascontiguousarray(x),
        "x_t": np.ascontiguousarray(x.T),
        "ctx_t": np.ascontiguousarray(a["ctx_1024"].reshape(B * SK, D).T),
        "columns": np.ascontiguousarray(np.concatenate([column(a[cols[k]]) for k in COLUMNS], axis=1)),
        "rows": np.ascontiguousarray(np.stack([rows[k] for k in ROWS])),
        "L0_wq": by_input(a["L0_xattn_Wq"]), "L0_wk": by_input(a["L0_xattn_Wk"]), "L0_wv": by_input(a["L0_xattn_Wv"]),
        "L0_w1": up(a["L0_xattn_W1"]), "L0_w2": by_input(a["L0_xattn_W2"]),
        "L1_wqkv": np.concatenate([by_input(qkv[i * D:(i + 1) * D]) for i in range(3)]),
        "L1_wproj": by_input(a["L1_xattn_attn_proj_w"]),
        "L1_wq": by_input(a["L1_xattn_q_w"]), "L1_wk": by_input(a["L1_xattn_k_w"]), "L1_wv": by_input(a["L1_xattn_v_w"]),
        "L1_wcaproj": by_input(a["L1_xattn_ca_proj_w"]),
        "L1_w1": up(a["L1_xattn_fc_w"]), "L1_w2": by_input(a["L1_xattn_proj_w"]),
    }


def kernel(**inputs):
    import concourse.bacc as bacc
    from concourse.bass_utils import run_bass_kernel_spmd

    arrays = lay_out(inputs)
    nc = bacc.Bacc("TRN2", target_bir_lowering=False, num_devices=1)
    d = {name: nc.dram_tensor(f"in_{name}", a.shape, mybir.dt.from_np(a.dtype), kind="ExternalInput").ap()
         for name, a in arrays.items()}
    d["out"] = nc.dram_tensor("out_y", (TOK, D), F32, kind="ExternalOutput").ap()
    build(nc, d)
    result = run_bass_kernel_spmd(nc, [{f"in_{name}": a for name, a in arrays.items()}], core_ids=[0])
    return result.results[0]["out_y"].reshape(B, S, D)
```

```python
from contextlib import ExitStack

import concourse.bass as bass
from concourse import mybir

F32 = mybir.dt.float32
F32R = mybir.dt.float32r
BF16 = mybir.dt.bfloat16
ALU = mybir.AluOpType
ACT = mybir.ActivationFunctionType
AX_X = mybir.AxisListType.X

P = 128
B, S, D = 2, 2048, 512
H = 16
DH = D // H
SK = 77
DFF = 2048
TOK = B * S
KT = D // P
G = D // P
HG = H // G
CH = 512
NCH = TOK // CH
TT = CH // P
FT = DFF // P
CPB = S // CH
KEYS = HG * SK
SCALE = float(DH) ** -0.5
EPS = 1e-5
MASKED = -1e30
BANK = 512


def wait(eng, sem, value):
    if not isinstance(value, int) or value > 0:
        eng.wait_ge(sem, value)


def over_chunks(eng, body, count=NCH, first=1, last=1):
    for n in range(first):
        body(n, n % 2, n // 2)
    with eng.Fori(0, (count - first - last) // 2) as i:
        for n in (first, first + 1):
            body(2 * i + n, n % 2, i + n // 2)
    for n in range(count - last, count):
        body(n, n % 2, n // 2)


def not_first(n):
    return not (isinstance(n, int) and n == 0)


def not_last(n, count=NCH):
    return not (isinstance(n, int) and n == count - 1)


def raw32(ap):
    return ap.bitcast(F32)


def mm3(pe, out, w_hi, w_lo, x_hi, x_lo, start, stop):
    pe.matmul(out, w_hi, x_hi, start=start, stop=False)
    pe.matmul(out, w_hi, x_lo, start=False, stop=False)
    return pe.matmul(out, w_lo, x_hi, start=False, stop=stop)


class Stage:

    def __init__(self, nc, tag, ctx):
        self.nc, self.tag, self.ctx, self.sems = nc, tag, ctx, []

    def sb(self, name, shape, dt=F32):
        return self.ctx.enter_context(self.nc.sbuf_tensor(f"{self.tag}_{name}", shape, dt))

    def psum(self, name, shape):
        return self.ctx.enter_context(self.nc.psum_tensor(f"{self.tag}_{name}", shape, F32))

    def sem(self, name):
        s = self.nc.alloc_semaphore(f"{self.tag}_{name}")
        self.sems.append(s)
        return s

    def close(self):
        self.nc.clear_and_free_semaphores(self.sems)
        self.nc.all_engine_barrier()



def build_constants(nc, ctx, c):
    def sb(name, shape, dt=F32):
        return ctx.enter_context(nc.sbuf_tensor(name, shape, dt))

    c["ident"] = sb("ident", [P, P])
    c["ident_bf"] = sb("ident_bf", [P, P], BF16)
    c["half_neg"] = sb("half_neg", [P, TT])
    c["eps"] = sb("eps", [P, TT])
    with ExitStack() as own:
        st = Stage(nc, "const", own)
        made = st.sem("made")
        with nc.Block() as block:
            @block.gpsimd
            def _(pool):
                pool.memset(c["ident"][:, :], 0.0).then_inc(made, 1)
                pool.wait_ge(made, 1)
                pool.affine_select(out=c["ident"][:, :], in_=c["ident"][:, :], compare_op=ALU.not_equal,
                                   fill=1.0, base=0, pattern=[[-1, P]], channel_multiplier=1).then_inc(made, 1)
                pool.wait_ge(made, 2)
                pool.tensor_copy(c["ident_bf"][:, :], c["ident"][:, :]).then_inc(made, 1)
                pool.memset(c["half_neg"][:, :], -0.5).then_inc(made, 1)
                pool.memset(c["eps"][:, :], EPS).then_inc(made, 1)
                pool.wait_ge(made, 5)
        st.close()



class LnTail:

    def __init__(self, st, c, gain, shift, out_t, ring=2):
        self.c, self.gain, self.shift, self.out_t = c, gain, shift, out_t
        self.stats = st.sb("stats", [P, TT, 6])
        self.mv = st.sb("mv", [P, TT, 2])
        self.veps = st.sb("veps", [P, TT, 1])
        self.rstd = st.sb("rstd", [P, TT])
        self.spacer = st.sb("spacer", [P, 1])
        self.z = st.sb("z", [P, TT, D])
        self.ring = ring
        self.out = st.sb("ln_out", [P, ring, CH])
        self.psum = st.psum("ln_psum", [P, ring, BANK])
        self.stats_made = st.sem("stats_made")
        self.mv_made = st.sem("mv_made")
        self.veps_made = st.sem("veps_made")
        self.rstd_made = st.sem("rstd_made")
        self.z_made = st.sem("z_made")
        self.turned = st.sem("turned")
        self.evacuated = st.sem("evacuated")
        self.stored = [st.sem(f"ln_stored{i}") for i in range(ring)]

    def dve_stats(self, dve, y, n):
        for t in range(TT):
            dve.bn_stats(self.stats[:, t, :], y[:, t, :]).then_inc(self.stats_made, 1)
        wait(dve, self.stats_made, n * TT + TT)
        dve.memset(self.spacer[:, :], 0.0)
        for t in range(TT):
            dve.bn_aggr(self.mv[:, t, :], self.stats[:, t, :]).then_inc(self.mv_made, 1)

    def pool_rstd(self, pool, n):
        wait(pool, self.mv_made, n * TT + TT)
        if not_first(n):
            wait(pool, self.z_made, n * TT)
        pool.tensor_tensor(self.veps[:, :, :], self.mv[:, :, 1:2], self.c["eps"][:, :].unsqueeze(2),
                           ALU.add).then_inc(self.veps_made, 1)
        wait(pool, self.veps_made, n + 1)
        pool.tensor_tensor(self.rstd[:, :], self.veps[:, :, 0], self.c["half_neg"][:, :],
                           ALU.pow).then_inc(self.rstd_made, 1)

    def dve_z(self, dve, y, n):
        wait(dve, self.rstd_made, n + 1)
        if not_first(n):
            wait(dve, self.turned, n * KT)
        for t in range(TT):
            dve.tensor_scalar(self.z[:, t, :], y[:, t, :], self.mv[:, t, 0:1], self.rstd[:, t:t + 1],
                              ALU.subtract, ALU.mult).then_inc(self.z_made, 1)

    def pe_turn(self, pe, n):
        wait(pe, self.z_made, n * TT + TT)
        for ft in range(KT):
            wait(pe, self.evacuated, n * KT + ft + 1)
            for t in range(TT):
                last = pe.transpose(self.psum[:, ft % self.ring, t * P:(t + 1) * P],
                                    self.z[:, t, ft * P:(ft + 1) * P], self.c["ident"][:, :])
            last.then_inc(self.turned, 1)

    def act_credit(self, act):
        act.sem_inc(self.evacuated, self.ring)

    def act_out(self, act, n):
        for ft in range(KT):
            wait(act, self.turned, n * KT + ft + 1)
            wait(act, self.stored[ft % self.ring], (n * (KT // self.ring) + ft // self.ring + 1) * 16)
            act.activation(self.out[:, ft % self.ring, :], self.psum[:, ft % self.ring, :], ACT.Identity,
                           bias=self.shift[:, ft:ft + 1],
                           scale=self.gain[:, ft:ft + 1]).then_inc(self.evacuated, 1)

    def store_credit(self, eng):
        for s in self.stored:
            eng.sem_inc(s, 16)

    def store(self, eng, n):
        for ft in range(KT):
            wait(eng, self.evacuated, n * KT + ft + self.ring + 1)
            eng.dma_start(self.out_t[:, ft, bass.ds(n * CH, CH)],
                          self.out[:, ft % self.ring, :]).then_inc(self.stored[ft % self.ring], 16)

    def drain(self, eng):
        for s in self.stored:
            eng.wait_ge(s, NCH * (KT // self.ring) * 16 + 16)


class SplitInput:

    def __init__(self, st, src, slots, slot_free, name="x", ring=2):
        self.src, self.slots, self.ring = src, slots, ring
        self.slot_free = slot_free
        self.raw = st.sb(f"{name}_raw", [P, ring, CH])
        self.hi = st.sb(f"{name}_hi", [P, slots, KT, CH], F32R)
        self.lo = st.sb(f"{name}_lo", [P, slots, KT, CH], F32R)
        self.loaded = [st.sem(f"{name}_loaded{i}") for i in range(ring)]
        self.hi_made = st.sem(f"{name}_hi_made")
        self.lo_made = st.sem(f"{name}_lo_made")

    def sp_load(self, sp, n, kts=range(KT)):
        for kt in kts:
            wait(sp, self.lo_made, n * KT + kt - self.ring + 3)
            sp.dma_start(self.raw[:, kt % self.ring, :],
                         self.src[:, kt, bass.ds(n * CH, CH)]).then_inc(self.loaded[kt % self.ring], 16)

    def make_hi(self, eng, copy, n, u, kts=range(KT)):
        if 0 in kts:
            self.slot_free(eng, n)
        for kt in kts:
            wait(eng, self.loaded[kt % self.ring], (n * (KT // self.ring) + kt // self.ring + 1) * 16)
            copy(self.hi[:, u % self.slots, kt, :], self.raw[:, kt % self.ring, :]).then_inc(self.hi_made, 1)

    def lo_credit(self, eng):
        eng.sem_inc(self.lo_made, 2)

    def make_lo(self, eng, n, u, kts=range(KT)):
        for kt in kts:
            wait(eng, self.hi_made, n * KT + kt + 1)
            eng.tensor_tensor(self.lo[:, u % self.slots, kt, :], self.raw[:, kt % self.ring, :],
                              raw32(self.hi[:, u % self.slots, kt, :]),
                              ALU.subtract).then_inc(self.lo_made, 1)

    def make_both(self, eng, n, u):
        for kt in range(KT):
            self.make_hi(eng, eng.tensor_copy, n, u, (kt,))
            self.make_lo(eng, n, u, (kt,))

    def pe_ready(self, pe, n):
        wait(pe, self.lo_made, n * KT + KT + 2)

    def halves(self, u, kt, cols):
        u = u % self.slots
        return self.hi[:, u, kt, cols], self.lo[:, u, kt, cols]


class Weights:
    PIECE = 512

    def __init__(self, st, pieces, name="w", ring=2, raw=None):
        self.pieces = pieces
        n = len(pieces)
        self.raw = st.sb(f"{name}_raw", [P, ring, self.PIECE]) if raw is None else raw
        self.ring = self.raw.shape[1]
        self.hi = st.sb(f"{name}_hi", [P, n, self.PIECE], F32R)
        self.lo = st.sb(f"{name}_lo", [P, n, self.PIECE], F32R)
        self.loaded = [st.sem(f"{name}_loaded{i}") for i in range(self.ring)]
        self.hi_made = st.sem(f"{name}_hi_made")
        self.lo_made = st.sem(f"{name}_lo_made")

    def sp_load(self, sp, first=0, last=None):
        for k in range(first, len(self.pieces) if last is None else last):
            wait(sp, self.lo_made, k - self.ring + 1)
            sp.dma_start(self.raw[:, k % self.ring, :], self.pieces[k]).then_inc(self.loaded[k % self.ring], 16)

    def hi_piece(self, eng, copy, k):
        eng.wait_ge(self.loaded[k % self.ring], (k // self.ring + 1) * 16)
        copy(self.hi[:, k, :], self.raw[:, k % self.ring, :]).then_inc(self.hi_made, 1)

    def lo_piece(self, eng, k):
        eng.wait_ge(self.hi_made, k + 1)
        eng.tensor_tensor(self.lo[:, k, :], self.raw[:, k % self.ring, :], raw32(self.hi[:, k, :]),
                          ALU.subtract).then_inc(self.lo_made, 1)

    def make_hi(self, eng, copy):
        for k in range(len(self.pieces)):
            self.hi_piece(eng, copy, k)

    def make_lo(self, eng):
        for k in range(len(self.pieces)):
            self.lo_piece(eng, k)

    def make_both(self, eng):
        for k in range(len(self.pieces)):
            self.hi_piece(eng, eng.tensor_copy, k)
            self.lo_piece(eng, k)

    def halves(self, k, cols=slice(0, 512)):
        return self.hi[:, k, cols], self.lo[:, k, cols]


def load_columns(nc, ctx, d, c):
    cols = ctx.enter_context(nc.sbuf_tensor("vector_columns", [P, d["columns"].shape[1]], F32))
    c["cols"] = cols
    with ExitStack() as own:
        st = Stage(nc, "cols", own)
        loaded = st.sem("loaded")
        with nc.Block() as block:
            @block.sync
            def _(sp):
                sp.dma_start(cols[:, :], d["columns"]).then_inc(loaded, 16)
                sp.wait_ge(loaded, 16)
        st.close()



def stage_ff(nc, tag, c, x_t, residual, w1, w2, b1, b2_row, y_out, norm=None):
    with ExitStack() as ctx:
        st = Stage(nc, tag, ctx)
        up_done = st.sem("up_done")
        x = SplitInput(st, x_t, 1, lambda eng, n: wait(eng, up_done, n * FT), ring=KT)
        w = Weights(st, [piece for j in range(FT) for piece in (w1[j], w2[j])])
        ln = LnTail(st, c, norm[0], norm[1], norm[2]) if norm else None
        act_out = st.sb("act_out", [P, 2, CH])
        h_hi = st.sb("h_hi", [P, 4, CH], F32R)
        h_lo = st.sb("h_lo", [P, 4, CH], F32R)
        y = st.sb("y", [P, 2, TT, D])
        b2 = st.sb("b2", [P, D])
        up = st.psum("up", [P, 2, BANK])
        acc = st.psum("acc", [P, TT, BANK])

        b2_loaded = st.sem("b2_loaded")
        res_loaded = [st.sem(f"res_loaded{i}") for i in range(2)]
        res_biased = st.sem("res_biased")
        gelu_done = st.sem("gelu_done")
        hi_done = st.sem("hi_done")
        lo_done = st.sem("lo_done")
        down_done = st.sem("down_done")
        y_done = st.sem("y_done")
        y_stored = [st.sem(f"y_stored{i}") for i in range(2)]

        with nc.Block() as block:
            @block.sync
            def _(sp):
                def load_residual(n, u, use):
                    wait(sp, y_stored[u], use * 16)
                    if ln and not (isinstance(n, int) and n < 2):
                        wait(sp, ln.z_made, (n - 1) * TT)
                    sp.dma_start(y[:, u], residual[:, bass.ds(n * TT, TT), :]).then_inc(res_loaded[u], 16)

                if ln:
                    ln.store_credit(sp)
                x.sp_load(sp, 0)
                w.sp_load(sp)
                sp.dma_start(b2[:, :], b2_row).then_inc(b2_loaded, 16)
                load_residual(0, 0, 0)

                def body(n, u, use):
                    if ln and not_first(n):
                        ln.store(sp, n - 1)
                    if not_last(n):
                        load_residual(n + 1, 1 - u, use + u)
                        x.sp_load(sp, n + 1)
                    wait(sp, y_done, n * TT + TT)
                    sp.dma_start(y_out[:, bass.ds(n * TT, TT), :], y[:, u]).then_inc(y_stored[u], 16)
                over_chunks(sp, body)
                if ln:
                    ln.store(sp, NCH - 1)
                    ln.drain(sp)
                for s in y_stored:
                    sp.wait_ge(s, NCH // 2 * 16)

            @block.gpsimd
            def _(pool):
                w.make_lo(pool)
                pool.wait_ge(b2_loaded, 16)

                def body(n, u, use):
                    wait(pool, res_loaded[u], (use + 1) * 16)
                    pool.tensor_tensor(y[:, u], y[:, u], b2[:, :].unsqueeze(1).to_broadcast([P, TT, D]),
                                       ALU.add).then_inc(res_biased, 1)
                    if ln and not_first(n):
                        ln.pool_rstd(pool, n - 1)
                over_chunks(pool, body)
                if ln:
                    ln.pool_rstd(pool, NCH - 1)

            @block.scalar
            def _(act):
                if ln:
                    ln.act_credit(act)

                for k in range(4):
                    w.hi_piece(act, act.copy, k)

                def body(n, u, use):
                    for j in range(FT):
                        if isinstance(n, int) and n == 0 and j < FT - 2:
                            for k in (2 * j + 4, 2 * j + 5):
                                w.hi_piece(act, act.copy, k)
                        wait(act, up_done, n * FT + j + 1)
                        wait(act, lo_done, n * FT + j - 1)
                        act.activation(act_out[:, j % 2, :], up[:, j % 2, :], ACT.Gelu,
                                       bias=b1[:, j:j + 1]).then_inc(gelu_done, 1)
                        if ln and j == 8 and not_first(n):
                            ln.act_out(act, n - 1)
                over_chunks(act, body)
                if ln:
                    ln.act_out(act, NCH - 1)

            @block.vector
            def _(dve):
                x.lo_credit(dve)
                x.make_both(dve, 0, 0)

                def body(n, u, use):
                    for j in range(FT):
                        wait(dve, gelu_done, n * FT + j + 1)
                        wait(dve, down_done, n * FT + j - 3)
                        dve.tensor_copy(h_hi[:, j % 4, :], act_out[:, j % 2, :]).then_inc(hi_done, 1)
                        wait(dve, hi_done, n * FT + j + 1)
                        dve.tensor_tensor(h_lo[:, j % 4, :], act_out[:, j % 2, :], raw32(h_hi[:, j % 4, :]),
                                          ALU.subtract).then_inc(lo_done, 1)
                        if ln and j == 1 and not_first(n):
                            ln.dve_stats(dve, y[:, 1 - u], n - 1)
                        if ln and j == 4 and not_first(n):
                            ln.dve_z(dve, y[:, 1 - u], n - 1)
                    if not_last(n):
                        x.make_both(dve, n + 1, 0)
                    wait(dve, down_done, n * FT + FT)
                    wait(dve, res_biased, n + 1)
                    for t in range(TT):
                        dve.tensor_tensor(y[:, u, t, :], acc[:, t, :], y[:, u, t, :], ALU.add).then_inc(y_done, 1)
                over_chunks(dve, body)
                if ln:
                    wait(dve, y_done, NCH * TT)
                    ln.dve_stats(dve, y[:, 1], NCH - 1)
                    ln.dve_z(dve, y[:, 1], NCH - 1)

            @block.tensor
            def _(pe):
                def up_tile(n, j):
                    if j == 0:
                        x.pe_ready(pe, n)
                    if isinstance(n, int) and n == 0:
                        wait(pe, w.lo_made, 2 * j + 1)
                    wait(pe, gelu_done, n * FT + j - 1)
                    for kt in range(KT):
                        last = mm3(pe, up[:, j % 2, :], *w.halves(2 * j, slice(kt * P, kt * P + P)),
                                   *x.halves(0, kt, slice(0, CH)), start=(kt == 0), stop=(kt == KT - 1))
                    last.then_inc(up_done, 1)

                def down_tile(n, j):
                    wait(pe, lo_done, n * FT + j + 1)
                    if isinstance(n, int) and n == 0:
                        wait(pe, w.lo_made, 2 * j + 2)
                    if j == 0:
                        wait(pe, y_done, n * TT)
                    for t in range(TT):
                        cols = slice(t * P, t * P + P)
                        last = mm3(pe, acc[:, t, :], h_hi[:, j % 4, cols], h_lo[:, j % 4, cols],
                                   *w.halves(2 * j + 1), start=(j == 0), stop=(j == FT - 1))
                    last.then_inc(down_done, 1)

                def body(n, u, use):
                    for j in range(FT):
                        up_tile(n, j)
                        if ln and j == 8 and not_first(n):
                            ln.pe_turn(pe, n - 1)
                        if j >= 2:
                            down_tile(n, j - 2)
                    down_tile(n, FT - 2)
                    down_tile(n, FT - 1)
                over_chunks(pe, body)
                if ln:
                    ln.pe_turn(pe, NCH - 1)
        st.close()



def stage_merge(nc, tag, c, att_t, residual, norm, y_out, w=None, bias_row=None, norm_rows=None):
    with ExitStack() as ctx:
        st = Stage(nc, tag, ctx)
        summed = st.sem("summed")
        ln = LnTail(st, c, norm[0], norm[1], norm[2], ring=KT)
        acc = st.psum("acc", [P, TT, BANK])
        res = st.sb("res", [P, 2, TT, D])
        y = st.sb("y", [P, 2, TT, D])
        row = st.sb("row", [P, 2, D])
        res_loaded = [st.sem(f"res_loaded{i}") for i in range(2)]
        row_loaded = st.sem("row_loaded")
        res_biased = st.sem("res_biased")
        y_done = st.sem("y_done")
        y_stored = [st.sem(f"y_stored{i}") for i in range(2)]
        if w is not None:
            x = SplitInput(st, att_t, 2, lambda eng, n: wait(eng, summed, n * TT + TT), ring=KT)
            weights = Weights(st, w, ring=KT)
        else:
            att = st.sb("att", [P, 2, KT, CH])
            att_loaded = [st.sem(f"att_loaded{i}") for i in range(2)]
        if norm_rows is not None:
            normed = st.sb("normed", [P, TT, D])
            gained = st.sem("gained")
            shifted = st.sem("shifted")
            normed_stored = st.sem("normed_stored")

        with nc.Block() as block:
            @block.sync
            def _(sp):
                def load_residual(n, u, use):
                    if not (isinstance(n, int) and n < 2):
                        wait(sp, y_done, (n - 1) * TT)
                    sp.dma_start(res[:, u], residual[:, bass.ds(n * TT, TT), :]).then_inc(res_loaded[u], 16)

                def load_att(n, u, use):
                    wait(sp, summed, n * TT + TT)
                    sp.dma_start(att[:, u], att_t[:, :, bass.ds(n * CH, CH)]).then_inc(att_loaded[u], 16)

                ln.store_credit(sp)
                rows = norm_rows if norm_rows is not None else (bias_row,)
                for r, src in enumerate(rows):
                    sp.dma_start(row[:, r, :], src).then_inc(row_loaded, 16)
                if w is not None:
                    weights.sp_load(sp)
                    x.sp_load(sp, 0)
                    x.sp_load(sp, 1)
                else:
                    load_att(0, 0, 0)
                load_residual(0, 0, 0)

                def body(n, u, use):
                    if not_last(n):
                        load_residual(n + 1, 1 - u, use + u)
                        if w is None:
                            load_att(n + 1, 1 - u, use + u)
                        elif not (isinstance(n, int) and n >= NCH - 2):
                            x.sp_load(sp, n + 2)
                over_chunks(sp, body, last=3)
                ln.drain(sp)
                if norm_rows is not None:
                    sp.wait_ge(normed_stored, NCH * 16)
                else:
                    for s in y_stored:
                        sp.wait_ge(s, NCH // 2 * 16)

            @block.gpsimd
            def _(pool):
                pool.wait_ge(row_loaded, 16 * (2 if norm_rows is not None else 1))
                if w is not None:
                    x.lo_credit(pool)
                    x.make_lo(pool, 0, 0)

                def bias_residual(n, u, use):
                    wait(pool, res_loaded[u], (use + 1) * 16)
                    pool.tensor_tensor(res[:, u], res[:, u], row[:, 0, :].unsqueeze(1).to_broadcast([P, TT, D]),
                                       ALU.add).then_inc(res_biased, 1)
                if w is not None:
                    bias_residual(0, 0, 0)

                def body(n, u, use):
                    if w is not None and not_first(n):
                        ln.pool_rstd(pool, n - 1)
                    if w is not None and not_last(n):
                        x.make_lo(pool, n + 1, 1 - u)
                        bias_residual(n + 1, 1 - u, use + u)
                    if w is None:
                        ln.pool_rstd(pool, n)
                    if norm_rows is not None:
                        wait(pool, ln.z_made, n * TT + TT)
                        wait(pool, normed_stored, n * 16)
                        pool.tensor_tensor(normed[:, :, :], ln.z[:, :, :],
                                           row[:, 0, :].unsqueeze(1).to_broadcast([P, TT, D]),
                                           ALU.mult).then_inc(gained, 1)
                over_chunks(pool, body)
                if w is not None:
                    ln.pool_rstd(pool, NCH - 1)

            @block.scalar
            def _(act):
                ln.act_credit(act)
                if w is not None:
                    weights.make_hi(act, act.copy)
                    x.make_hi(act, act.copy, 0, 0)

                def body(n, u, use):
                    if w is not None and not_last(n):
                        x.make_hi(act, act.copy, n + 1, 1 - u)
                    if not_first(n):
                        leave(n - 1)
                    if norm_rows is None:
                        wait(act, y_done, n * TT + TT)
                        act.dma_start(y_out[:, bass.ds(n * TT, TT), :], y[:, u]).then_inc(y_stored[u], 16)

                def leave(n):
                    ln.act_out(act, n)
                    ln.store(act, n)
                    if norm_rows is not None:
                        wait(act, shifted, n + 1)
                        act.dma_start(y_out[:, bass.ds(n * TT, TT), :],
                                      normed[:, :, :]).then_inc(normed_stored, 16)
                over_chunks(act, body)
                leave(NCH - 1)

            @block.vector
            def _(dve):
                if w is not None:
                    weights.make_lo(dve)

                def body(n, u, use):
                    if w is not None:
                        wait(dve, res_biased, n + 1)
                    else:
                        wait(dve, res_loaded[u], (use + 1) * 16)
                    if norm_rows is None:
                        wait(dve, y_stored[u], use * 16)
                    for t in range(TT):
                        wait(dve, summed, 2 * TT + n * TT + t + 1)
                        dve.tensor_tensor(y[:, u, t, :], acc[:, t, :], res[:, u, t, :], ALU.add).then_inc(y_done, 1)
                    wait(dve, y_done, n * TT + TT)
                    ln.dve_stats(dve, y[:, u], n)
                    if norm_rows is not None and not_first(n):
                        shift_rows(n - 1)
                    ln.dve_z(dve, y[:, u], n)

                def shift_rows(n):
                    wait(dve, gained, n + 1)
                    dve.tensor_tensor(normed[:, :, :], normed[:, :, :],
                                      row[:, 1, :].unsqueeze(1).to_broadcast([P, TT, D]),
                                      ALU.add).then_inc(shifted, 1)
                over_chunks(dve, body)
                if norm_rows is not None:
                    shift_rows(NCH - 1)

            @block.tensor
            def _(pe):
                pe.sem_inc(summed, 2 * TT)
                if w is not None:
                    pe.wait_ge(weights.lo_made, len(w))

                def body(n, u, use):
                    if w is not None:
                        x.pe_ready(pe, n)
                    else:
                        wait(pe, att_loaded[u], (use + 1) * 16)
                    for t in range(TT):
                        cols = slice(t * P, t * P + P)
                        wait(pe, y_done, (n - 1) * TT + t + 1)
                        for kt in range(KT):
                            if w is not None:
                                last = mm3(pe, acc[:, t, :], *x.halves(u, kt, cols), *weights.halves(kt),
                                           start=(kt == 0), stop=(kt == KT - 1))
                            else:
                                last = pe.transpose(acc[:, t, kt * P:kt * P + P], att[:, u, kt, cols],
                                                    c["ident"][:, :])
                        last.then_inc(summed, 1)
                        if t == 2 and not_first(n):
                            ln.pe_turn(pe, n - 1)
                over_chunks(pe, body)
                ln.pe_turn(pe, NCH - 1)
        st.close()



def stage_qkv(nc, tag, c, x_t, w, bias_cols, v_row, qk_out, v_out):
    with ExitStack() as ctx:
        st = Stage(nc, tag, ctx)
        tiles = 3 * KT
        done = st.sem("done")
        x = SplitInput(st, x_t, 2, lambda eng, n: wait(eng, done, n * tiles + tiles), ring=KT)
        weights = Weights(st, w, ring=KT)
        acc = st.psum("acc", [P, 4, BANK])
        hi = st.sb("hi", [P, 2, 2, KT, CH], F32R)
        lo = st.sb("lo", [P, 2, 2, KT, CH], F32R)
        v = st.sb("v", [P, TT, D])
        row = st.sb("row", [P, D])
        row_loaded = st.sem("row_loaded")
        hi_out = st.sem("hi_out")
        lo_out = st.sem("lo_out")
        v_done = st.sem("v_done")
        qk_stored = [[st.sem(f"qk_stored{i}{k}") for k in range(4)] for i in range(2)]
        v_stored = st.sem("v_stored")
        with nc.Block() as block:
            @block.sync
            def _(sp):
                sp.dma_start(row[:, :], v_row).then_inc(row_loaded, 16)
                weights.sp_load(sp, 0, KT)
                x.sp_load(sp, 0)
                weights.sp_load(sp, KT)
                x.sp_load(sp, 1)

                def body(n, u, use):
                    if not (isinstance(n, int) and n >= NCH - 2):
                        x.sp_load(sp, n + 2)
                    for kind in range(4):
                        if kind % 2 == 0:
                            wait(sp, lo_out, n * 8 + 4 + 2 * kind)
                        tile = (hi, lo)[kind % 2]
                        sp.dma_start(qk_out[kind][:, :, bass.ds(n * CH, CH)],
                                     raw32(tile[:, u, kind // 2])).then_inc(qk_stored[u][kind], 16)
                    wait(sp, v_done, n * TT + TT)
                    sp.dma_start(v_out[:, bass.ds(n * TT, TT), :], v[:, :, :]).then_inc(v_stored, 16)
                over_chunks(sp, body, last=3)
                for s in qk_stored[0] + qk_stored[1]:
                    sp.wait_ge(s, NCH // 2 * 16)
                sp.wait_ge(v_stored, NCH * 16)

            @block.gpsimd
            def _(pool):
                x.lo_credit(pool)
                x.make_lo(pool, 0, 0)

                def body(n, u, use):
                    if not_last(n):
                        x.make_lo(pool, n + 1, 1 - u)
                over_chunks(pool, body)

            @block.scalar
            def _(act):
                for k in range(KT):
                    weights.hi_piece(act, act.copy, k)
                x.make_hi(act, act.copy, 0, 0)
                for k in range(KT, 3 * KT):
                    weights.hi_piece(act, act.copy, k)

                def body(n, u, use):
                    if not_last(n):
                        x.make_hi(act, act.copy, n + 1, 1 - u)
                    for f in range(8):
                        if f % KT == 0:
                            wait(act, qk_stored[u][2 * (f // KT)], use * 16)
                        wait(act, done, 2 * tiles + n * tiles + f + 1)
                        act.activation(hi[:, u, f // KT, f % KT, :], acc[:, f % 4, :], ACT.Identity,
                                       bias=bias_cols[:, f:f + 1]).then_inc(hi_out, 1)
                over_chunks(act, body)

            @block.vector
            def _(dve):
                weights.make_lo(dve)
                dve.wait_ge(row_loaded, 16)

                def body(n, u, use):
                    for f in range(8):
                        if f % KT == 0:
                            wait(dve, qk_stored[u][2 * (f // KT) + 1], use * 16)
                        wait(dve, hi_out, n * 8 + f + 1)
                        dve.scalar_tensor_tensor(out=lo[:, u, f // KT, f % KT, :], in0=acc[:, f % 4, :],
                                                 scalar=bias_cols[:, f:f + 1],
                                                 in1=raw32(hi[:, u, f // KT, f % KT, :]),
                                                 op0=ALU.add, op1=ALU.subtract).then_inc(lo_out, 1)
                    wait(dve, v_stored, n * 16)
                    for t in range(TT):
                        wait(dve, done, 2 * tiles + n * tiles + 8 + t + 1)
                        dve.tensor_tensor(v[:, t, :], acc[:, t, :], row[:, :], ALU.add).then_inc(v_done, 1)
                over_chunks(dve, body)

            @block.tensor
            def _(pe):
                pe.sem_inc(done, 2 * tiles)
                def body(n, u, use):
                    x.pe_ready(pe, n)
                    for f in range(8):
                        if isinstance(n, int) and n == 0 and f % KT == 0:
                            pe.wait_ge(weights.lo_made, f + KT)
                        if f < 4:
                            wait(pe, v_done, (n - 1) * TT + f + 1)
                        else:
                            wait(pe, lo_out, n * 8 + f - 3)
                        for kt in range(KT):
                            cols = slice((f % KT) * P, (f % KT) * P + P)
                            last = mm3(pe, acc[:, f % 4, :], *weights.halves((f // KT) * KT + kt, cols),
                                       *x.halves(u, kt, slice(0, CH)), start=(kt == 0), stop=(kt == KT - 1))
                        last.then_inc(done, 1)
                    if isinstance(n, int) and n == 0:
                        pe.wait_ge(weights.lo_made, 3 * KT)
                    for t in range(TT):
                        wait(pe, lo_out, n * 8 + 5 + t)
                        for kt in range(KT):
                            last = mm3(pe, acc[:, t, :], *x.halves(u, kt, slice(t * P, t * P + P)),
                                       *weights.halves(2 * KT + kt), start=(kt == 0), stop=(kt == KT - 1))
                        last.then_inc(done, 1)
                over_chunks(pe, body)
        st.close()



def stage_cross(nc, tag, c, x_t, wq, q_bias, ctx_t, wk, k_bias, wv, v_bias, att_out, causal):
    with ExitStack() as ctx:
        st = Stage(nc, tag, ctx)
        k_hi = st.sb("k_hi", [P, B, G, KEYS], F32R)
        k_lo = st.sb("k_lo", [P, B, G, KEYS], F32R)
        v = st.sb("v", [SK, B, D])
        mask32 = st.sb("mask32", [P, SK])
        mask = st.sb("mask", [P, NCH, SK], BF16)
        probs_t = st.sb("probs_t", [P, 2, H, CH])
        wk_sb = probs_t[:, 0, 0:KT, :]
        wv_sb = probs_t[:, 0, KT:2 * KT, :]
        ctx_sb = probs_t[:, 1, 0:KT, 0:B * SK]
        ctx_loaded = st.sem("ctx_loaded")
        wv_loaded = st.sem("wv_loaded")
        zeroed = st.sem("zeroed")
        mask_made = st.sem("mask_made")
        k_summed = st.sem("k_summed")
        v_summed = st.sem("v_summed")
        k_hi_done = st.sem("k_hi_done")
        k_lo_done = st.sem("k_lo_done")
        v_done = st.sem("v_done")

        q_done = st.sem("q_done")
        x = SplitInput(st, x_t, 2, lambda eng, n: wait(eng, q_done, (n - 1) * G), ring=KT)
        weights = Weights(st, wq, raw=probs_t[:, 1, KT:2 * KT, :])
        q_hi = st.sb("q_hi", [P, 2, G, CH], F32R)
        q_lo = st.sb("q_lo", [P, 2, G, CH], F32R)
        e = st.sb("e", [P, TT, H, SK])
        v_now = st.sb("v_now", [SK, 2, D])
        biggest = st.sb("biggest", [P, H])
        shift = st.sb("shift", [P, H])
        total = st.sb("total", [P, 2, H])
        inverse = st.sb("inverse", [P, 2, H])
        att = st.sb("att", [P, 2, CH])
        scores = st.psum("scores", [P, G, BANK])
        qp = st.psum("qp", [P, BANK])
        turned_p = st.psum("turned_p", [P, 2, BANK])
        att_p = st.psum("att_p", [P, BANK])
        scored = st.sem("scored")
        q_hi_done = st.sem("q_hi_done")
        q_lo_done = st.sem("q_lo_done")
        max_done = st.sem("max_done")
        shift_done = st.sem("shift_done")
        exp_done = st.sem("exp_done")
        inverse_done = st.sem("inverse_done")
        probs_done = st.sem("probs_done")
        turned = st.sem("turned")
        left = st.sem("left")
        v_ready = st.sem("v_ready")
        weighed = st.sem("weighed")
        att_done = st.sem("att_done")
        att_stored = [st.sem(f"att_stored{i}") for i in range(2)]
        last_m = NCH * TT - 1

        def steps(body):
            def chunk(n, u, use):
                for t in range(TT):
                    body(n * TT + t, n, t, u, use)
            return chunk

        def ago(m, n, t, u, lag):
            if isinstance(m, int) and m < lag:
                return None
            return (m - lag, n, t - lag, u) if t >= lag else (m - lag, n - 1, t - lag + TT, 1 - u)

        def there(n):
            return not (isinstance(n, int) and n >= NCH)

        def next_x(n, t, u):
            piece = (n + 2, t + 1, u) if t < TT - 1 else (n + 3, 0, 1 - u)
            return piece if there(piece[0]) else None

        def next_q(n, t, u):
            piece = (n + 1, t + 1, 1 - u) if t < TT - 1 else (n + 2, 0, u)
            return piece if there(piece[0]) else None

        def weighed_at(n, t, u):
            piece = (n - 1, t - 2, 1 - u) if t >= 2 else (n - 2, t + 2, u)
            return None if isinstance(n, int) and piece[0] < 0 else piece

        LAST = [(NCH - 2, 2, None), (NCH - 2, 3, qp[:, :])] + [(NCH - 1, g, scores[:, g, :]) for g in range(G)]

        def before(n, t, u):
            return (n, t - 1, u) if t > 0 else (n - 1, TT - 1, 1 - u)

        with nc.Block() as block:
            @block.sync
            def _(sp):
                sp.dma_start(ctx_sb, ctx_t).then_inc(ctx_loaded, 16)
                for kt in range(KT):
                    sp.dma_start(wk_sb[:, kt, :], wk[kt]).then_inc(ctx_loaded, 16)
                for kt in range(KT):
                    sp.dma_start(wv_sb[:, kt, :], wv[kt]).then_inc(wv_loaded, 16)
                x.sp_load(sp, 0)
                weights.sp_load(sp)
                x.sp_load(sp, 1)
                x.sp_load(sp, 2, (0,))

                def store(n, groups):
                    for g in groups:
                        wait(sp, att_done, n * G + g + 2)
                        sp.dma_start(att_out[:, g, bass.ds(n * CH, CH)], att[:, g % 2]).then_inc(att_stored[g % 2], 16)

                def body(n, u, use):
                    for t in range(TT):
                        piece = next_x(n, t, u)
                        if piece:
                            x.sp_load(sp, piece[0], piece[1:2])
                    if not (isinstance(n, int) and n < 2):
                        store(n - 2, (2, 3))
                    if not_first(n):
                        store(n - 1, (0, 1))
                for n in range(NCH):
                    body(n, n % 2, n // 2)
                store(NCH - 2, (2, 3))
                store(NCH - 1, range(G))
                for s in att_stored:
                    sp.wait_ge(s, NCH * G // 2 * 16)

            @block.gpsimd
            def _(pool):
                x.lo_credit(pool)
                pool.memset(mask[:, :, :], 0.0).then_inc(mask_made, 1)
                if causal:
                    pool.memset(mask32[:, :], 0.0).then_inc(mask_made, 1)
                    pool.wait_ge(mask_made, 2)
                    pool.affine_select(out=mask32[:, :], in_=mask32[:, :], compare_op=ALU.is_ge,
                                       fill=MASKED, base=0, pattern=[[-1, SK]],
                                       channel_multiplier=1).then_inc(mask_made, 1)
                    pool.wait_ge(mask_made, 3)
                    for b in range(B):
                        pool.tensor_copy(mask[:, b * CPB, :], mask32[:, :]).then_inc(mask_made, 1)
                for n in range(2):
                    x.make_lo(pool, n, n)
                x.make_lo(pool, 2, 0, (0,))

                def normalize(m, n, t, u):
                    wait(pool, inverse_done, m + 1)
                    pool.tensor_tensor(e[:, t], e[:, t],
                                       inverse[:, t % 2, :].unsqueeze(2).to_broadcast([P, H, SK]),
                                       ALU.mult).then_inc(probs_done, 1)

                def body(m, n, t, u, use):
                    past = ago(m, n, t, u, 1)
                    if past:
                        normalize(*past)
                    piece = next_x(n, t, u)
                    if piece:
                        x.make_lo(pool, piece[0], piece[2], piece[1:2])
                over_chunks(pool, steps(body), last=3)
                normalize(last_m, NCH - 1, TT - 1, 1)

            @block.scalar
            def _(act):
                act.wait_ge(zeroed, 2)
                for g in range(G):
                    act.wait_ge(k_summed, g + 1)
                    for h in range(HG):
                        part = slice(h * DH, h * DH + DH)
                        act.activation(k_hi[part, :, g, h * SK:h * SK + SK],
                                       scores[part, g, 0:B * SK].rearrange("p (b k) -> p b k", b=B),
                                       ACT.Identity, bias=k_bias[part, g:g + 1]).then_inc(k_hi_done, 1)
                x.make_hi(act, act.copy, 0, 0)
                weights.make_hi(act, act.copy)
                x.make_hi(act, act.copy, 1, 1)

                def q_out(k, n, g, u, bank=qp[:, :]):
                    wait(act, q_done, k + 1)
                    act.activation(q_hi[:, u, g, :], bank, ACT.Identity,
                                   bias=q_bias[:, g:g + 1]).then_inc(q_hi_done, 1)

                for g in range(G):
                    q_out(g, 0, g, 0, scores[:, g, :])

                def body(m, n, t, u, use):
                    if not_last(n) and not_first(m):
                        q_out((n + 1) * G + t, n + 1, t, 1 - u)
                    wait(act, turned, (m - 3) * G)
                    wait(act, inverse_done, m - 1)
                    for g in range(G):
                        wait(act, shift_done, m * G + g + 1)
                        for h in range(g * HG, g * HG + HG):
                            last = act.activation(e[:, t, h, :], scores[:, g, (h % HG) * SK:(h % HG) * SK + SK],
                                                  ACT.Exp, bias=shift[:, h:h + 1], scale=SCALE,
                                                  accum_out=total[:, t % 2, h:h + 1])
                        last.then_inc(exp_done, 1)
                    if not not_first(m):
                        q_out(G, 1, 0, 1)
                        x.make_hi(act, act.copy, 2, 0, (0,))
                    piece = next_x(n, t, u)
                    if piece:
                        x.make_hi(act, act.copy, piece[0], piece[2], piece[1:2])
                over_chunks(act, steps(body), last=3)

            @block.vector
            def _(dve):
                dve.memset(raw32(k_hi[:, :, :, :]), 0.0).then_inc(zeroed, 1)
                dve.memset(raw32(k_lo[:, :, :, :]), 0.0).then_inc(zeroed, 1)
                for g in range(G):
                    for h in range(HG):
                        part = slice(h * DH, h * DH + DH)
                        dve.wait_ge(k_hi_done, g * HG + h + 1)
                        keys = slice(h * SK, h * SK + SK)
                        dve.scalar_tensor_tensor(
                            out=k_lo[part, :, g, keys],
                            in0=scores[part, g, 0:B * SK].rearrange("p (b k) -> p b k", b=B),
                            scalar=k_bias[part, g:g + 1], in1=raw32(k_hi[part, :, g, keys]),
                            op0=ALU.add, op1=ALU.subtract).then_inc(k_lo_done, 1)
                weights.make_lo(dve)
                for b in range(B):
                    dve.wait_ge(v_summed, b + 1)
                    dve.tensor_copy(v[:, b, :], turned_p[0:SK, b, :]).then_inc(v_done, 1)
                dve.wait_ge(v_done, B)
                dve.sem_inc(att_done, 1)

                def invert(m, n, t, u):
                    wait(dve, exp_done, m * G + G)
                    wait(dve, probs_done, m - 1)
                    dve.reciprocal(inverse[:, t % 2, :], total[:, t % 2, :]).then_inc(inverse_done, 1)

                def att_leave(n, g, bank=None):
                    wait(dve, att_stored[g % 2], 16 * (n * 2 + g // 2))
                    wait(dve, weighed, 2 * G + n * G + g + 1)
                    dve.tensor_scalar(att[:, g % 2, :], att_p[:, :] if bank is None else bank, v_bias[:, g:g + 1], None,
                                      ALU.add).then_inc(att_done, 1)

                def q_out(k, n, g, u, bank=qp[:, :]):
                    wait(dve, q_hi_done, k + 1)
                    dve.scalar_tensor_tensor(out=q_lo[:, u, g, :], in0=bank, scalar=q_bias[:, g:g + 1],
                                             in1=raw32(q_hi[:, u, g, :]), op0=ALU.add,
                                             op1=ALU.subtract).then_inc(q_lo_done, 1)

                def maxima(m, g):
                    hs = slice(g * HG, g * HG + HG)
                    wait(dve, scored, m * G + g + 1)
                    dve.tensor_reduce(biggest[:, hs], scores[:, g, 0:KEYS].rearrange("p (h k) -> p h k", h=HG),
                                      AX_X, ALU.max).then_inc(max_done, 1)
                    wait(dve, max_done, m * G + g + 1)
                    dve.tensor_scalar(shift[:, hs], biggest[:, hs], -SCALE, None, ALU.mult).then_inc(shift_done, 1)

                def leave(m, n, t, u, g):
                    if g == 0 and t == 0:
                        wait(dve, weighed, (n + 1) * G)
                    wait(dve, turned, m * G + g + 1)
                    dve.tensor_copy(probs_t[0:SK, u, g * HG:g * HG + HG, t * P:t * P + P],
                                    turned_p[0:SK, g % 2, :].rearrange("k (h q) -> k h q", h=HG)).then_inc(left, 1)

                for g in range(G):
                    q_out(g, 0, g, 0, scores[:, g, :])

                def body(m, n, t, u, use):
                    past, older = ago(m, n, t, u, 1), ago(m, n, t, u, 2)
                    weighed_before = weighed_at(*before(n, t, u))
                    if weighed_before:
                        att_leave(*weighed_before[:2])
                    if t == 2:
                        wait(dve, weighed, (n + 1) * G)
                        dve.tensor_copy(v_now[:, u, :],
                                        v[:, bass.ds(n // CPB, 1), :]).then_inc(v_ready, 1)
                    for g in range(G):
                        maxima(m, g)
                        if g == (0 if not_first(m) else G - 1) and not_last(n):
                            q_out((n + 1) * G + t, n + 1, t, 1 - u)
                        if g == 1 and past:
                            invert(*past)
                        if g < 2 and older:
                            leave(*older, g)
                    for g in (2, 3):
                        if older:
                            leave(*older, g)
                over_chunks(dve, steps(body), first=2, last=2)
                invert(last_m, NCH - 1, TT - 1, 1)
                for t in (TT - 2, TT - 1):
                    for g in range(G):
                        leave(last_m - TT + 1 + t, NCH - 1, t, 1, g)
                att_leave(*weighed_at(NCH - 1, TT - 1, 1)[:2])
                for n, g, bank in LAST:
                    att_leave(n, g, bank)

            @block.tensor
            def _(pe):
                pe.sem_inc(weighed, 2 * G)
                pe.wait_ge(ctx_loaded, 16 * (1 + KT))
                for g in range(G):
                    for kt in range(KT):
                        last = pe.matmul(scores[:, g, 0:B * SK], wk_sb[:, kt, g * P:g * P + P], ctx_sb[:, kt, :],
                                         start=(kt == 0), stop=(kt == KT - 1))
                    last.then_inc(k_summed, 1)
                pe.wait_ge(wv_loaded, 16 * KT)
                for b in range(B):
                    for kt in range(KT):
                        last = pe.matmul(turned_p[0:SK, b, :], ctx_sb[:, kt, b * SK:b * SK + SK], wv_sb[:, kt, :],
                                         start=(kt == 0), stop=(kt == KT - 1))
                    last.then_inc(v_summed, 1)
                pe.wait_ge(weights.lo_made, len(wq))

                def project(n, g, u, bank=None):
                    if g == 0:
                        x.pe_ready(pe, n)
                    if bank is None:
                        bank = qp[:, :]
                        wait(pe, q_lo_done, n * G + g)
                    for kt in range(KT):
                        last = mm3(pe, bank, *weights.halves(kt, slice(g * P, g * P + P)),
                                   *x.halves(u, kt, slice(0, CH)), start=(kt == 0), stop=(kt == KT - 1))
                    last.then_inc(q_done, 1)

                def score(m, n, t, u, g):
                    wait(pe, exp_done, (m - 1) * G + g + 1)
                    if t == 0:
                        wait(pe, q_lo_done, n * G + g + 1)
                    cols = slice(t * P, t * P + P)
                    at = (slice(None), bass.ds(n // CPB, 1), g)
                    masked = causal and t == 0
                    last = mm3(pe, scores[:, g, 0:KEYS], q_hi[:, u, g, cols], q_lo[:, u, g, cols],
                               k_hi[at], k_lo[at], start=True, stop=not masked)
                    if masked:
                        last = pe.matmul(scores[:, g, 0:KEYS], c["ident_bf"][:, :],
                                         mask[:, bass.ds(n, 1), :].to_broadcast([P, HG, SK]),
                                         start=False, stop=True)
                    last.then_inc(scored, 1)

                def turn(m, n, t, u, g):
                    if g == 0:
                        wait(pe, probs_done, m + 1)
                    wait(pe, left, m * G + g - 1)
                    for h in range(HG):
                        last = pe.transpose(turned_p[0:SK, g % 2, h * P:h * P + P],
                                            e[:, t, g * HG + h, :], c["ident"][:, :])
                    last.then_inc(turned, 1)

                def weigh(n, g, u, bank=None):
                    wait(pe, v_ready, n + 1)
                    wait(pe, left, (n + 1) * TT * G)
                    if bank is None:
                        bank = att_p[:, :]
                        wait(pe, att_done, n * G + g + 1)
                    for h in range(HG):
                        head = g * HG + h
                        last = pe.matmul(bank[h * DH:h * DH + DH, :],
                                         v_now[:, u, head * DH:head * DH + DH], probs_t[0:SK, u, head, :],
                                         start=True, stop=True)
                    last.then_inc(weighed, 1)

                pe.wait_ge(k_lo_done, H)
                for g in range(G):
                    project(0, g, 0, scores[:, g, :])
                pe.wait_ge(v_done, B)
                pe.wait_ge(mask_made, 3 + B if causal else 1)

                def body(m, n, t, u, use):
                    older = ago(m, n, t, u, 2)
                    ready = weighed_at(n, t, u)
                    for g in range(G):
                        score(m, n, t, u, g)
                        if g < 2 and older:
                            turn(*older, g)
                    if older:
                        turn(*older, 2)
                    if ready:
                        weigh(*ready)
                    if older:
                        turn(*older, 3)
                    if not not_first(m):
                        project(1, 0, 1)
                    piece = next_q(n, t, u)
                    if piece:
                        project(*piece)
                over_chunks(pe, steps(body), first=2, last=2)
                for t in (TT - 2, TT - 1):
                    for g in range(G):
                        turn(last_m - TT + 1 + t, NCH - 1, t, 1, g)
                for n, g, bank in LAST:
                    weigh(n, g, n % 2, bank)
        st.close()



def stage_self(nc, tag, c, qk, v_in, att_out):
    NQ = S // CH
    NW = B * G
    STACK = 3 * DH
    units = [TT * (q + 1) for q in range(NQ)]
    first_unit = [sum(units[:q]) for q in range(NQ)]
    UNITS = sum(units)
    PT = 4
    first_pair = [sum(q_ * TT // 2 for q_ in range(q)) for q in range(NQ)]
    PAIRS = sum(q * TT // 2 for q in range(NQ))

    LAG = 10
    items, rows_due = [], []
    for q in range(NQ):
        for h in range(HG):
            for t in range(TT):
                for block_ in range(q + 1):
                    items.append(("scores", q, h, t, block_))
                    if rows_due and len(items) >= rows_due[0][0]:
                        items.append(rows_due.pop(0)[1])
            rows_due.append((len(items) + LAG, ("row", q, h)))
    items += [row for _, row in rows_due]
    ITEMS = len(items)
    MP = 4
    assert ITEMS % MP == 0
    row_at = {(it[1], it[2]): i for i, it in enumerate(items) if it[0] == "row"}
    BEFORE = row_at[0, HG - 1] + 1
    STEADY = ITEMS * 2 // 5

    def lot(w, g):
        rest = first_unit[NQ - 1]
        done = {rest - 1: ITEMS - 1, rest: ITEMS, UNITS: ITEMS + STEADY}
        if not_first(w):
            done[0] = STEADY
        else:
            done[0] = BEFORE
            for q in range(1, NQ - 1):
                done[first_unit[q]] = row_at[q, HG - 1] + 1
        marks = sorted(done)

        def by(unit):
            at = max(m for m in marks if m <= unit)
            if at == UNITS:
                return done[UNITS]
            to = min(m for m in marks if m > unit)
            return done[at] + (done[to] - done[at]) * (unit - at) // (to - at)
        for q in range(1, NQ):
            assert by(first_unit[q]) > row_at[q, HG - 1]
        span = range(by(g), by(g + 1))
        return [i for i in span if i < ITEMS or not_last(w, NW)]

    def parts(w, g):
        todo = lot(w, g)
        return [todo[len(todo) * k // 4:len(todo) * (k + 1) // 4] for k in range(4)]

    with ExitStack() as ctx:
        st = Stage(nc, tag, ctx)
        ks = st.sb("ks", [P, 2, HG, S], F32R)
        qs = st.sb("qs", [P, 2, HG, S], F32R)
        v = st.sb("v", [P, 2, S // P, P])
        pt = st.sb("pt", [P, PT, HG, CH])
        pair_sum = st.sb("pair_sum", [P, 2, HG, CH])
        diag = st.sb("diag", [P, HG, CH], F32R)
        ones_r = st.sb("ones_r", [P, P], F32R)
        ones = st.sb("ones", [P, DH])
        mask32 = st.sb("mask32", [P, P])
        mask_q = st.sb("mask_q", [P, P], BF16)
        mask_k = st.sb("mask_k", [P, P], BF16)
        part_max = st.sb("part_max", [P, HG, TT, NQ])
        neg_max = st.sb("neg_max", [P, HG, TT])
        total = st.sb("total", [P, CH])
        att = st.sb("att", [P, CH])
        sc = st.psum("sc", [P, 2, BANK])
        mp = st.psum("mp", [P, MP, BANK])
        out = st.psum("out", [P, BANK])
        den = st.psum("den", [P, BANK])

        const_made = st.sem("const_made")
        ready = st.sem("ready")
        ones_set = st.sem("ones_set")
        part_loaded = [st.sem(f"part_loaded{i}") for i in range(NQ)]
        v_loaded = st.sem("v_loaded")
        k_loaded = [st.sem(f"k_loaded{i}") for i in range(2)]
        item_done = st.sem("item_done")
        item_read = st.sem("item_read")
        max_done = st.sem("max_done")
        diag_done = st.sem("diag_done")
        scored = st.sem("scored")
        exp_done = st.sem("exp_done")
        half_added = st.sem("half_added")
        unit_done = st.sem("unit_done")
        left = st.sem("left")
        inverse_done = st.sem("inverse_done")
        att_done = st.sem("att_done")
        att_stored = st.sem("att_stored")

        OPERANDS = ((ks, 0, 2), (qs, 0, 0), (ks, 1, 2), (qs, 1, 1), (ks, 2, 3), (qs, 2, 0))

        def over_pairs(eng, body):
            over_chunks(eng, body, NW)

        def chunk_number(w, q):
            return w * NQ + q

        def unit_number(w, q, k):
            return w * UNITS + first_unit[q] + k

        def pair_number(w, q, k):
            return w * PAIRS + first_pair[q] + k // 2

        def before(w, u, q, k):
            if k > 0:
                return w, u, q, k - 1
            if q > 0:
                return w, u, q - 1, units[q - 1] - 1
            return (w - 1, 1 - u, NQ - 1, units[NQ - 1] - 1) if not_first(w) else None

        def width_of(q, t, block_):
            return min(CH, (q * TT + t + 1) * P - block_ * CH)

        with nc.Block() as block:
            @block.sync
            def _(sp):
                def load(w, u):
                    wait(sp, unit_done, (w - 1) * UNITS)
                    b, g = w // G, w % G
                    toks = bass.ds(b * S, S)

                    for dst, part, kind in OPERANDS:
                        src = qk[kind][:, bass.ds(g, 1), toks].rearrange("(h r) o t -> r (h o) t", r=DH)
                        sp.dma_start(raw32(dst[part * DH:part * DH + DH, u]), src).then_inc(k_loaded[u], 16)
                    sp.dma_start(v[:, u], v_in[:, bass.ds(b * (S // P), S // P),
                                               bass.ds(g * P, P)]).then_inc(k_loaded[u], 16)
                for q in range(NQ):
                    toks = slice(q * CH, q * CH + CH)
                    for dst, part, kind in OPERANDS:
                        src = qk[kind][:, 0:1, toks].rearrange("(h r) o t -> r (h o) t", r=DH)
                        sp.dma_start(raw32(dst[part * DH:part * DH + DH, 0, :, toks]),
                                     src).then_inc(part_loaded[q], 16)
                    if q == 0:
                        sp.dma_start(v[:, 0], v_in[:, 0:S // P, 0:P]).then_inc(v_loaded, 16)

                def body(w, u, use):
                    if not_last(w, NW):
                        load(w + 1, 1 - u)
                    b, g = w // G, w % G
                    for q in range(NQ):
                        wait(sp, att_done, chunk_number(w, q) + 1)
                        sp.dma_start(att_out[:, bass.ds(g, 1), bass.ds(b * S + q * CH, CH)],
                                     att[:, :].unsqueeze(1)).then_inc(att_stored, 16)
                over_pairs(sp, body)
                sp.wait_ge(att_stored, NW * NQ * 16)

            @block.gpsimd
            def _(pool):
                pool.memset(mask32[:, :], 0.0).then_inc(const_made, 1)
                pool.wait_ge(const_made, 1)
                pool.affine_select(out=mask32[:, :], in_=mask32[:, :], compare_op=ALU.is_ge, fill=MASKED,
                                   base=0, pattern=[[-1, P]], channel_multiplier=1).then_inc(const_made, 1)
                pool.wait_ge(const_made, 2)
                pool.tensor_copy(mask_q[:, :], mask32[:, :]).then_inc(const_made, 1)
                pool.wait_ge(const_made, 3)
                pool.memset(mask32[:, :], 0.0).then_inc(const_made, 1)
                pool.wait_ge(const_made, 4)
                pool.affine_select(out=mask32[:, :], in_=mask32[:, :], compare_op=ALU.is_ge, fill=MASKED,
                                   base=0, pattern=[[1, P]], channel_multiplier=-1).then_inc(const_made, 1)
                pool.wait_ge(const_made, 5)
                pool.tensor_copy(mask_k[:, :], mask32[:, :]).then_inc(const_made, 1)

                def spread(w, i):
                    kind, q, h, *at = items[i]
                    if kind == "row" or at != [TT - 1, q]:
                        return
                    if q > 0:
                        wait(pool, item_done, w * ITEMS + row_at[q - 1, h] + 1)
                    elif not_first(w):
                        wait(pool, item_done, (w - 1) * ITEMS + row_at[NQ - 1, h] + 1)
                    wait(pool, max_done, chunk_number(w, q) * HG + h + 1)
                    pool.tensor_tensor(diag[:, h, :].rearrange("p (t q) -> p t q", t=TT),
                                       c["ident"][:, :].unsqueeze(1).to_broadcast([P, TT, P]),
                                       neg_max[:, h, :].unsqueeze(2).to_broadcast([P, TT, P]),
                                       ALU.mult).then_inc(diag_done, 1)

                def leave(w, q):
                    wait(pool, inverse_done, (chunk_number(w, q) + 1) * TT)
                    pool.tensor_tensor(att[:, :], att[:, :], total[:, :], ALU.mult).then_inc(att_done, 1)

                def add_pair(w, q, a, half):
                    hs = slice(2 * half, 2 * half + 2)
                    if half == 0:
                        wait(pool, unit_done, unit_number(w, q, a) if a >= 4 else unit_number(w, q, 0) - 1)
                    wait(pool, exp_done, unit_number(w, q, a + 1) * HG + 2 * half + 2)
                    pool.tensor_tensor(pair_sum[:, a // 2 % 2, hs, :], pt[:, a % PT, hs, :],
                                       pt[:, (a + 1) % PT, hs, :], ALU.add).then_inc(half_added, 1)

                for i in range(BEFORE):
                    spread(0, i)

                def body(w, u, use):
                    for q in range(NQ):
                        for k in range(units[q]):
                            if 2 <= k < q * TT + 2:
                                add_pair(w, q, k // 2 * 2 - 2, k % 2)
                            for i in lot(w, first_unit[q] + k):
                                if i < ITEMS:
                                    spread(w, i)
                                else:
                                    spread(w + 1, i - ITEMS)
                            past = before(w, u, q, 0)
                            if k == 2 and past:
                                leave(past[0], past[2])
                over_pairs(pool, body)
                leave(NW - 1, NQ - 1)

            @block.vector
            def _(dve):
                dve.memset(raw32(ones_r[:, :]), 1.0).then_inc(ready, 1)
                dve.memset(ones[:, :], 1.0).then_inc(ready, 1)

                def read(w, u, base, lot_):
                    for i in lot_:
                        kind, q, h, *at = items[i]
                        wait(dve, item_done, base + i + 1)
                        if kind == "row":
                            dve.tensor_copy(qs[STACK:STACK + 1, u, h, q * CH:q * CH + CH],
                                            mp[STACK:STACK + 1, i % MP, :]).then_inc(item_read, 1)
                            continue
                        t, block_ = at
                        dve.tensor_reduce(part_max[:, h, t, block_:block_ + 1],
                                          mp[:, i % MP, 0:width_of(q, t, block_)],
                                          AX_X, ALU.max).then_inc(item_read, 1)
                        if (t, block_) == (TT - 1, q):
                            wait(dve, diag_done, (chunk_number(w, q) - 1) * HG + h + 1)
                            wait(dve, item_read, base + i + 1)
                            dve.tensor_reduce(neg_max[:, h, :], part_max[:, h, :, 0:q + 1], AX_X, ALU.max,
                                              negate=True).then_inc(max_done, 1)
                read(0, 0, 0, range(BEFORE))

                def invert(w, q, t):
                    wait(dve, left, chunk_number(w, q) * 2 + 2)
                    cols = slice(t * P, t * P + P)
                    dve.reciprocal(total[:, cols], total[:, cols]).then_inc(inverse_done, 1)

                def body(w, u, use):
                    for q in range(NQ):
                        for k in range(units[q]):
                            past = before(w, u, q, 0)
                            for part, lot_ in enumerate(parts(w, first_unit[q] + k)):
                                for i in lot_:
                                    if i < ITEMS:
                                        read(w, u, w * ITEMS, [i])
                                    else:
                                        read(w + 1, 1 - u, (w + 1) * ITEMS, [i - ITEMS])
                                if k in (1, 2) and part % 2 and past:
                                    invert(past[0], past[2], (k - 1) * 2 + part // 2)
                over_pairs(dve, body)
                for t in range(TT):
                    invert(NW - 1, NQ - 1, t)

            @block.scalar
            def _(act):
                act.wait_ge(ready, 2)
                for slot in range(2):
                    act.copy(ks[STACK:STACK + 1, slot], ones[STACK:STACK + 1, 0:1].unsqueeze(2)
                             .to_broadcast([1, HG, S])).then_inc(ones_set, 1)

                def leave(w, q):
                    wait(act, unit_done, unit_number(w, q, units[q]))
                    wait(act, att_stored, chunk_number(w, q) * 16)
                    act.copy(att[:, :], out[:, :]).then_inc(left, 1)
                    act.copy(total[:, :], den[:, :]).then_inc(left, 1)

                def body(w, u, use):
                    for q in range(NQ):
                        for k in range(units[q]):
                            number = unit_number(w, q, k)
                            start = max(0, k - q * TT) * P
                            wait(act, unit_done, number - PT + 1)
                            for h in range(HG):
                                if PT <= k < q * TT + PT and h % 2 == 0:
                                    wait(act, half_added, pair_number(w, q, k - PT) * 2 + h // 2 + 1)
                                wait(act, scored, number * HG + h + 1)
                                act.activation(pt[:, k % PT, h, start:CH], sc[:, h % 2, start:CH], ACT.Exp,
                                               scale=SCALE).then_inc(exp_done, 1)
                            past = before(w, u, q, k)
                            if k == 0 and past:
                                leave(past[0], past[2])
                over_pairs(act, body)
                leave(NW - 1, NQ - 1)

            @block.tensor
            def _(pe):
                def run_items(w, u, base, lot_):
                    for i in lot_:
                        kind, q, h, *at = items[i]
                        if isinstance(w, int) and w == 0 and (kind, h, *at) == ("scores", 0, 0, 0):
                            wait(pe, part_loaded[q], len(OPERANDS) * 16)
                        if kind == "row":
                            wait(pe, diag_done, chunk_number(w, q) * HG + h + 1)
                            wait(pe, item_read, base + i + 1 - MP)
                            pe.matmul(mp[:, i % MP, :], ones_r[:, :], diag[:, h, :],
                                      start=True, stop=True).then_inc(item_done, 1)
                            continue
                        t, block_ = at
                        width = width_of(q, t, block_)
                        tile = (q * TT + t) * P
                        wait(pe, item_read, base + i + 1 - MP)
                        last = pe.matmul(mp[:, i % MP, 0:width], qs[0:STACK, u, h, tile:tile + P],
                                         ks[0:STACK, u, h, block_ * CH:block_ * CH + width],
                                         start=True, stop=block_ < q)
                        if block_ == q:
                            last = pe.matmul(mp[:, i % MP, width - P:width], c["ident_bf"][:, :], mask_q[:, :],
                                             start=False, stop=True)
                        last.then_inc(item_done, 1)

                def score(w, u, q, k, h):
                    number = unit_number(w, q, k)
                    start = max(0, k - q * TT) * P
                    diagonal = k >= q * TT
                    if k == 0:
                        wait(pe, item_read, w * ITEMS + row_at[q, h] + 1)
                    wait(pe, exp_done, number * HG + h - 1)
                    last = pe.matmul(sc[:, h % 2, start:CH], ks[0:STACK + 1, u, h, k * P:k * P + P],
                                     qs[0:STACK + 1, u, h, q * CH + start:q * CH + CH],
                                     start=True, stop=not diagonal)
                    if diagonal:
                        last = pe.matmul(sc[:, h % 2, start:start + P], c["ident_bf"][:, :],
                                         mask_k[:, :], start=False, stop=True)
                    last.then_inc(scored, 1)

                def weigh(w, u, q, k):
                    number = unit_number(w, q, k)
                    start = max(0, k - q * TT) * P
                    if k == 0:
                        wait(pe, left, chunk_number(w, q) * 2)
                    wait(pe, exp_done, number * HG + HG)
                    for h in range(HG):
                        part = slice(h * DH, h * DH + DH)
                        last = pe.matmul(out[part, start:CH], v[:, u, k, part], pt[:, k % PT, h, start:CH],
                                         start=(k == 0), stop=(k == units[q] - 1))
                    return last

                def add_up(w, u, q, k):
                    start = max(0, k - q * TT) * P
                    for h in range(HG):
                        part = slice(h * DH, h * DH + DH)
                        last = pe.matmul(den[part, start:CH], ones[:, :], pt[:, k % PT, h, start:CH],
                                         start=(k == 0), stop=(k == units[q] - 1))
                    return last

                def add_up_pair(w, q, a):
                    wait(pe, half_added, pair_number(w, q, a) * 2 + 2)
                    for h in range(HG):
                        last = pe.matmul(den[h * DH:h * DH + DH, :], ones[:, :], pair_sum[:, a // 2 % 2, h, :],
                                         start=(a == 0), stop=False)
                    return last

                pe.wait_ge(ready, 2)
                pe.wait_ge(const_made, 6)
                run_items(0, 0, 0, range(BEFORE))
                pe.wait_ge(v_loaded, 16)
                pe.wait_ge(ones_set, 2)

                def body(w, u, use):
                    for q in range(NQ):
                        for k in range(units[q]):
                            past = before(w, u, q, k)
                            diagonal = past is not None and past[3] >= past[2] * TT
                            paired = 4 <= k < q * TT + 4 and k % 2 == 0
                            for part, lot_ in enumerate(parts(w, first_unit[q] + k)):
                                if part == 2 and past:
                                    last = weigh(*past)
                                    if not (diagonal or paired):
                                        last.then_inc(unit_done, 1)
                                score(w, u, q, k, part)
                                for i in lot_:
                                    if i == ITEMS:
                                        wait(pe, k_loaded[1 - u], (use + 1) * (len(OPERANDS) + 1) * 16)
                                    if i < ITEMS:
                                        run_items(w, u, w * ITEMS, [i])
                                    else:
                                        run_items(w + 1, 1 - u, (w + 1) * ITEMS, [i - ITEMS])
                            if paired:
                                last = add_up_pair(w, q, k - 4)
                            if diagonal:
                                last = add_up(*past)
                            if diagonal or paired:
                                last.then_inc(unit_done, 1)
                over_pairs(pe, body)
                weigh(NW - 1, 1, NQ - 1, units[NQ - 1] - 1)
                add_up(NW - 1, 1, NQ - 1, units[NQ - 1] - 1).then_inc(unit_done, 1)
        st.close()



COLUMNS = {}
for _name, _n in (("L0_bq", 4), ("L0_bk", 4), ("L0_bv", 4), ("L0_ln_g", 4), ("L0_ln_b", 4), ("L0_b1", FT),
                  ("L1_ln1_g", 4), ("L1_ln1_b", 4), ("L1_qkv_b", 12), ("L1_ln2_g", 4), ("L1_ln2_b", 4),
                  ("L1_q_b", 4), ("L1_k_b", 4), ("L1_v_b", 4), ("L1_ln3_g", 4), ("L1_ln3_b", 4), ("L1_fc_b", FT)):
    COLUMNS[_name] = (sum(n for _, n in COLUMNS.values()), _n)
ROWS = ("L0_ln_g", "L0_ln_b", "L0_b2", "L1_v_b", "L1_attn_proj_b", "L1_ca_proj_b", "L1_proj_b")


def build(nc, d):
    def features(ap):
        return ap.rearrange("(k p) t -> p k t", p=P)

    def tokens(ap):
        return ap.rearrange("(n p) d -> p n d", p=P)

    def scratch(name, shape):
        return nc.dram_tensor(name, shape, F32, kind="Internal").ap()

    def pieces(name):
        return [d[name][k] for k in range(d[name].shape[0])]

    def row(name):
        r = ROWS.index(name)
        return d["rows"][r:r + 1, :].to_broadcast([P, D])

    att_t = features(scratch("att_t", (D, TOK)))
    att2_t = features(scratch("att2_t", (D, TOK)))
    norm_t = features(scratch("norm_t", (D, TOK)))
    norm2_t = features(scratch("norm2_t", (D, TOK)))
    y_a = tokens(scratch("y_a", (TOK, D)))
    y_b = tokens(scratch("y_b", (TOK, D)))
    v_all = tokens(scratch("v_all", (TOK, D)))
    qk = [features(scratch(f"qk{k}", (D, TOK))) for k in range(4)]

    with ExitStack() as ctx:
        c = {}
        build_constants(nc, ctx, c)
        load_columns(nc, ctx, d, c)

        def col(name):
            first, n = COLUMNS[name]
            return c["cols"][:, first:first + n]

        stage_cross(nc, "ca0", c, features(d["x_t"]), pieces("L0_wq"), col("L0_bq"), features(d["ctx_t"]),
                    pieces("L0_wk"), col("L0_bk"), pieces("L0_wv"), col("L0_bv"), att_t, causal=True)
        stage_merge(nc, "ln0", c, att_t, tokens(d["x"]), (col("L0_ln_g"), col("L0_ln_b"), norm_t), y_a,
                    norm_rows=(row("L0_ln_g"), row("L0_ln_b")))
        stage_ff(nc, "ff0", c, norm_t, y_a, pieces("L0_w1"), pieces("L0_w2"), col("L0_b1"), row("L0_b2"), y_b,
                 (col("L1_ln1_g"), col("L1_ln1_b"), norm2_t))
        stage_qkv(nc, "qkv", c, norm2_t, pieces("L1_wqkv"), col("L1_qkv_b"), row("L1_v_b"), qk, v_all)
        stage_self(nc, "sa", c, qk, v_all, att2_t)
        stage_merge(nc, "pr1", c, att2_t, y_b, (col("L1_ln2_g"), col("L1_ln2_b"), norm_t), y_a,
                    w=pieces("L1_wproj"), bias_row=row("L1_attn_proj_b"))
        stage_cross(nc, "ca1", c, norm_t, pieces("L1_wq"), col("L1_q_b"), features(d["ctx_t"]),
                    pieces("L1_wk"), col("L1_k_b"), pieces("L1_wv"), col("L1_v_b"), att_t, causal=False)
        stage_merge(nc, "pr2", c, att_t, y_a, (col("L1_ln3_g"), col("L1_ln3_b"), norm2_t), y_b,
                    w=pieces("L1_wcaproj"), bias_row=row("L1_ca_proj_b"))
        stage_ff(nc, "ff1", c, norm2_t, y_b, pieces("L1_w1"), pieces("L1_w2"), col("L1_fc_b"),
                 row("L1_proj_b"), tokens(d["out"]))


def lay_out(inputs):
    import numpy as np
    a = {k: np.asarray(v) for k, v in inputs.items()}

    def by_input(w):
        return np.ascontiguousarray(w.T.reshape(w.shape[1] // P, P, w.shape[0]))

    def up(w):
        return np.ascontiguousarray(w.T.reshape(KT, P, FT, P).transpose(2, 1, 0, 3).reshape(FT, P, D))

    def column(v):
        return v.reshape(-1, P).T

    cols = {"L0_bq": "L0_xattn_bq", "L0_bk": "L0_xattn_bk", "L0_bv": "L0_xattn_bv", "L0_ln_g": "L0_xattn_ln_g",
            "L0_ln_b": "L0_xattn_ln_b", "L0_b1": "L0_xattn_b1", "L1_ln1_g": "L1_xattn_ln1_g",
            "L1_ln1_b": "L1_xattn_ln1_b", "L1_qkv_b": "L1_xattn_attn_qkv_b", "L1_ln2_g": "L1_xattn_ln2_g",
            "L1_ln2_b": "L1_xattn_ln2_b", "L1_q_b": "L1_xattn_q_b", "L1_k_b": "L1_xattn_k_b",
            "L1_v_b": "L1_xattn_v_b", "L1_ln3_g": "L1_xattn_ln3_g", "L1_ln3_b": "L1_xattn_ln3_b",
            "L1_fc_b": "L1_xattn_fc_b"}
    rows = {"L0_ln_g": a["L0_xattn_ln_g"], "L0_ln_b": a["L0_xattn_ln_b"], "L0_b2": a["L0_xattn_b2"],
            "L1_v_b": a["L1_xattn_attn_qkv_b"][2 * D:], "L1_attn_proj_b": a["L1_xattn_attn_proj_b"],
            "L1_ca_proj_b": a["L1_xattn_ca_proj_b"], "L1_proj_b": a["L1_xattn_proj_b"]}
    x = a["x"].reshape(TOK, D)
    qkv = a["L1_xattn_attn_qkv_w"]
    return {
        "x": np.ascontiguousarray(x),
        "x_t": np.ascontiguousarray(x.T),
        "ctx_t": np.ascontiguousarray(a["ctx_1024"].reshape(B * SK, D).T),
        "columns": np.ascontiguousarray(np.concatenate([column(a[cols[k]]) for k in COLUMNS], axis=1)),
        "rows": np.ascontiguousarray(np.stack([rows[k] for k in ROWS])),
        "L0_wq": by_input(a["L0_xattn_Wq"]), "L0_wk": by_input(a["L0_xattn_Wk"]), "L0_wv": by_input(a["L0_xattn_Wv"]),
        "L0_w1": up(a["L0_xattn_W1"]), "L0_w2": by_input(a["L0_xattn_W2"]),
        "L1_wqkv": np.concatenate([by_input(qkv[i * D:(i + 1) * D]) for i in range(3)]),
        "L1_wproj": by_input(a["L1_xattn_attn_proj_w"]),
        "L1_wq": by_input(a["L1_xattn_q_w"]), "L1_wk": by_input(a["L1_xattn_k_w"]),
        "L1_wv": by_input(a["L1_xattn_v_w"]),
        "L1_wcaproj": by_input(a["L1_xattn_ca_proj_w"]),
        "L1_w1": up(a["L1_xattn_fc_w"]), "L1_w2": by_input(a["L1_xattn_proj_w"]),
    }


def kernel(**inputs):
    import concourse.bacc as bacc
    from concourse.bass_utils import run_bass_kernel_spmd

    arrays = lay_out(inputs)
    nc = bacc.Bacc("TRN2", target_bir_lowering=False, num_devices=1)
    d = {name: nc.dram_tensor(f"in_{name}", a.shape, mybir.dt.from_np(a.dtype), kind="ExternalInput").ap()
         for name, a in arrays.items()}
    d["out"] = nc.dram_tensor("out_y", (TOK, D), F32, kind="ExternalOutput").ap()
    build(nc, d)
    result = run_bass_kernel_spmd(nc, [{f"in_{name}": a for name, a in arrays.items()}], core_ids=[0])
    return result.results[0]["out_y"].reshape(B, S, D)
```
